# Optimizing a Trainium2 kernel written in Bass

```python
import numpy as np
import jax
import jax.numpy as jnp

def _softmax(x, axis=-1):
    return jax.nn.softmax(x, axis=axis)

def _gelu(x):
    return jax.nn.gelu(x, approximate=True)

def _silu(x):
    return jax.nn.silu(x)

def _sigmoid(x):
    return jax.nn.sigmoid(x)

def _layernorm(x, axis=-1, eps=1e-05):
    m = jnp.mean(x, axis=axis, keepdims=True)
    v = jnp.var(x, axis=axis, keepdims=True)
    return (x - m) / jnp.sqrt(v + eps)

def _scatter_add(tgt, idx, src, axis=0):
    return tgt.at[idx].add(src)

def _segment_sum(src, seg, n):
    return jax.ops.segment_sum(src, seg, n)
kernel_name = 'mk_vit_tower_postln_d1_tok_img768_r4_d5e3ba'

def setup_inputs(seed: int=0):
    np.random.seed(seed)
    _w = jnp.asarray

    def _rec_inputs():
        import jax
        import jax.numpy as jnp
        _rk = jax.random.key(seed)
        x = -0.000356955 + 1 * jax.random.normal(jax.random.fold_in(_rk, 1), (64, 3, 96, 96), jnp.float32)
        return x
    x = _rec_inputs()

    def _L0_tok_setup():
        import jax, jax.numpy as jnp
        import numpy as np
        IMAGE_SIZE = 224
        PATCH = 16
        HIDDEN = 192
        C = 3
        key = jax.random.key(seed)
        k1, k2, k3 = jax.random.split(key, 3)
        img = jax.random.normal(k1, (128, C, IMAGE_SIZE, IMAGE_SIZE), dtype=jnp.float32)
        d_in = C * PATCH * PATCH
        bound = 1.0 / np.sqrt(d_in)
        W = jax.random.uniform(k2, (HIDDEN, d_in), jnp.float32, -bound, bound)
        b = jax.random.uniform(k3, (HIDDEN,), jnp.float32, -bound, bound)
        return {'img': img, 'W': W, 'b': b}
    _L0_tok_all = _L0_tok_setup()
    _L0_tok_in = {k: v for k, v in _L0_tok_all.items() if k in ('W', 'b')}
    del _L0_tok_all

    def _L0_attn_setup():
        import jax, jax.numpy as jnp
        import numpy as np
        B, N, C, H = (4, 512, 192, 12)
        D = C // H
        SCALE = D ** (-0.5)
        key = jax.random.key(seed)
        k1, k2, k3 = jax.random.split(key, 3)
        x = jax.random.normal(k1, (B, N, C), dtype=jnp.float32)
        w_qkv = jax.random.normal(k2, (C, 3 * C), dtype=jnp.float32) * 0.02
        w_proj = jax.random.normal(k3, (C, C), dtype=jnp.float32) * 0.02
        b_proj = jnp.zeros((C,), dtype=jnp.float32)
        temperature = jnp.ones((H, 1, 1), dtype=jnp.float32) * 0.5
        return {'x': x, 'w_qkv': w_qkv, 'w_proj': w_proj, 'b_proj': b_proj, 'temperature': temperature}
    _L0_attn_all = _L0_attn_setup()
    _L0_attn_in = {k: v for k, v in _L0_attn_all.items() if k in ('w_qkv', 'w_proj', 'b_proj', 'temperature')}
    del _L0_attn_all

    def _L0_ffn_setup():
        import jax, jax.numpy as jnp
        import numpy as np
        D = 192
        I = 768
        E = 8
        K = 2
        LIMIT = 10.0
        VOCAB = 8192

        def _expert(xf, W1, W2, W3):
            gate = jnp.minimum(xf @ W1, LIMIT)
            up = jnp.clip(xf @ W3, -LIMIT, LIMIT)
            return jax.nn.silu(gate) * up @ W2
        key = jax.random.key(seed)
        ks = jax.random.split(key, 10)
        s = 0.02
        return {'x': jax.random.normal(ks[0], (1, 512, D), dtype=jnp.float32), 'input_ids': jax.random.randint(ks[1], (1, 512), 0, VOCAB, dtype=jnp.int64), 'gate_w': jax.random.normal(ks[2], (D, E), dtype=jnp.float32) * s, 'gate_bias': jnp.zeros((E,), dtype=jnp.float32), 'w1': jax.random.normal(ks[3], (E, D, I), dtype=jnp.float32) * s, 'w2': jax.random.normal(ks[4], (E, I, D), dtype=jnp.float32) * s, 'w3': jax.random.normal(ks[5], (E, D, I), dtype=jnp.float32) * s, 'w1s': jax.random.normal(ks[6], (D, I), dtype=jnp.float32) * s, 'w2s': jax.random.normal(ks[7], (I, D), dtype=jnp.float32) * s, 'w3s': jax.random.normal(ks[8], (D, I), dtype=jnp.float32) * s}
    _L0_ffn_all = _L0_ffn_setup()
    _L0_ffn_in = {k: v for k, v in _L0_ffn_all.items() if k in ('input_ids', 'gate_w', 'gate_bias', 'w1', 'w2', 'w3', 'w1s', 'w2s', 'w3s')}
    del _L0_ffn_all
    return {'x': x, 'L0_tok_W': _L0_tok_in['W'], 'L0_tok_b': _L0_tok_in['b'], 'L0_attn_w_qkv': _L0_attn_in['w_qkv'], 'L0_attn_w_proj': _L0_attn_in['w_proj'], 'L0_attn_b_proj': _L0_attn_in['b_proj'], 'L0_attn_temperature': _L0_attn_in['temperature'], 'L0_ffn_input_ids': _L0_ffn_in['input_ids'], 'L0_ffn_gate_w': _L0_ffn_in['gate_w'], 'L0_ffn_gate_bias': _L0_ffn_in['gate_bias'], 'L0_ffn_w1': _L0_ffn_in['w1'], 'L0_ffn_w2': _L0_ffn_in['w2'], 'L0_ffn_w3': _L0_ffn_in['w3'], 'L0_ffn_w1s': _L0_ffn_in['w1s'], 'L0_ffn_w2s': _L0_ffn_in['w2s'], 'L0_ffn_w3s': _L0_ffn_in['w3s']}

def reference(x, L0_tok_W, L0_tok_b, L0_attn_w_qkv, L0_attn_w_proj, L0_attn_b_proj, L0_attn_temperature, L0_ffn_input_ids, L0_ffn_gate_w, L0_ffn_gate_bias, L0_ffn_w1, L0_ffn_w2, L0_ffn_w3, L0_ffn_w1s, L0_ffn_w2s, L0_ffn_w3s):
    import jax
    import jax.numpy as jnp

    def _L0_tok_ref(img, W, b):
        import jax, jax.numpy as jnp
        import numpy as np
        IMAGE_SIZE = 224
        PATCH = 16
        HIDDEN = 192
        C = 3
        B, Cc, H, Wd = img.shape
        hp, wp = (H // PATCH, W // PATCH if False else Wd // PATCH)
        hp = H // PATCH
        x = img.reshape(B, Cc, hp, PATCH, wp, PATCH)
        x = x.transpose(0, 2, 4, 1, 3, 5)
        x = x.reshape(B, hp * wp, Cc * PATCH * PATCH)
        return jnp.einsum('bld,hd->blh', x, W) + b

    def _L0_attn_ref(x, w_qkv, w_proj, b_proj, temperature):
        import jax, jax.numpy as jnp
        import numpy as np
        B, N, C, H = (4, 512, 192, 12)
        D = C // H
        SCALE = D ** (-0.5)
        b, n, c = x.shape
        h, d = (H, c // H)
        qkv = (x @ w_qkv).reshape(b, n, 3, h, d)
        q, k, v = jnp.moveaxis(qkv, 2, 0)
        q = q.transpose(0, 2, 1, 3)
        k = k.transpose(0, 2, 1, 3)
        v = v.transpose(0, 2, 1, 3)
        attn = jnp.einsum('bhnd,bhmd->bhnm', q, k) * SCALE
        eye = jnp.eye(n, dtype=attn.dtype)
        attn = attn * (1.0 - temperature[None] * eye)
        attn = jax.nn.softmax(attn, axis=-1)
        out = jnp.einsum('bhnm,bhmd->bhnd', attn, v)
        out = out.transpose(0, 2, 1, 3).reshape(b, n, c)
        return out @ w_proj + b_proj

    def _L0_ffn_ref(x, input_ids, gate_w, gate_bias, w1, w2, w3, w1s, w2s, w3s):
        import jax, jax.numpy as jnp
        import numpy as np
        D = 192
        I = 768
        E = 8
        K = 2
        LIMIT = 10.0
        VOCAB = 8192

        def _expert(xf, W1, W2, W3):
            gate = jnp.minimum(xf @ W1, LIMIT)
            up = jnp.clip(xf @ W3, -LIMIT, LIMIT)
            return jax.nn.silu(gate) * up @ W2
        B, T, _ = x.shape
        flat = x.reshape(-1, D)
        N = flat.shape[0]
        scores = jnp.sqrt(jax.nn.softplus(flat @ gate_w))
        routed_scores = scores + gate_bias
        _, indices = jax.lax.top_k(routed_scores, K)
        weights = jnp.take_along_axis(scores, indices, axis=1)
        weights = weights / jnp.clip(weights.sum(axis=-1, keepdims=True), 1e-06)
        combine = jnp.zeros((N, E), dtype=weights.dtype)
        combine = combine.at[jnp.arange(N)[:, None], indices].add(weights)
        y = _expert(flat, w1s, w2s, w3s)
        gate_h = jnp.minimum(jnp.einsum('td,edi->eti', flat, w1), LIMIT)
        up_h = jnp.clip(jnp.einsum('td,edi->eti', flat, w3), -LIMIT, LIMIT)
        h = jax.nn.silu(gate_h) * up_h
        out_e = jnp.einsum('eti,eid->etd', h, w2)
        routed = jnp.einsum('etd,te->td', out_e, combine)
        return (y + routed).reshape(B, T, D)
    h = _L0_tok_ref(x, L0_tok_W, L0_tok_b)
    h = _layernorm(h + _L0_attn_ref(h, L0_attn_w_qkv, L0_attn_w_proj, L0_attn_b_proj, L0_attn_temperature), axis=-1)
    h = _layernorm(h + _L0_ffn_ref(h, L0_ffn_input_ids, L0_ffn_gate_w, L0_ffn_gate_bias, L0_ffn_w1, L0_ffn_w2, L0_ffn_w3, L0_ffn_w1s, L0_ffn_w2s, L0_ffn_w3s), axis=-1)
    return h

_drawn_inputs = setup_inputs


def setup_inputs(seed=0):
    import zlib

    import numpy as np

    out = dict(_drawn_inputs(seed))
    spreads = {'L0_attn_b_proj': (0.0, 0.1),
     'L0_attn_temperature': (0.5, 0.6),
     'L0_ffn_gate_bias': (0.0, 0.51)}
    factors = {'L0_attn_w_qkv': 4.354,
     'L0_attn_w_proj': 4.45,
     'L0_ffn_gate_w': 5.397,
     'L0_ffn_w1': 3.711,
     'L0_ffn_w2': 3.677,
     'L0_ffn_w3': 3.674,
     'L0_ffn_w1s': 3.535,
     'L0_ffn_w2s': 3.529,
     'L0_ffn_w3s': 3.521}
    for name, (base, spread) in spreads.items():
        noise = np.random.default_rng([zlib.crc32(name.encode()), seed]).standard_normal(out[name].shape)
        drawn = base * np.exp(spread * noise) if base else spread * noise
        out[name] = jnp.asarray(drawn.astype(out[name].dtype))
    for name, factor in factors.items():
        out[name] = (out[name] * factor).astype(out[name].dtype)
    return out
```

```python
from contextlib import ExitStack

import numpy as np

import concourse.bass as bass
from concourse import mybir

ALU = mybir.AluOpType
ACT = mybir.ActivationFunctionType
AX = mybir.AxisListType
F32 = mybir.dt.float32
I32 = mybir.dt.int32

IMAGES, CHAN, SIDE, PATCH = 64, 3, 96, 16
GRID = SIDE // PATCH
N = GRID * GRID
TOKENS = IMAGES * N
D_IN = CHAN * PATCH * PATCH
C = 192
KI = D_IN // 128
HC = C // 2
HEADS, HD = 12, 16
HH = 3
TRIPLES = HEADS // HH
RT = 64 + HH * HD
ROWS = HH * N
G = 8
GT = G * N
GROUPS = IMAGES // G
TM = 96
TILES = TOKENS // TM
GTILES = GT // TM
E, I = 8, 768
IC = I // 128
UPF = 2 * 2 * I
WF = UPF + IC * C
XT = 128
SHT = TOKENS // XT
RTILES = (2 * TOKENS + E * (XT - 1)) // XT
ALLT = SHT + RTILES
XROWS = ALLT * XT
SCALE = HD ** -0.5
EPS = 1e-5
LIMIT = 10.0
SILU_LIMIT = LIMIT / (1.0 + float(np.exp(-LIMIT)))
BIG = 1e30
ROUTE_SOFTPLUS, ROUTE_CHOICES = 11, 24

def _columns(fields):
    at, out = 0, {}
    for name, width in fields:
        out[name] = (at, at + width)
        at += width
    return out, at


PAR, PAR_W = _columns([
    ("wtok", KI * C), ("wq", 2 * 2 * RT), ("wk", 2 * 2 * RT), ("wv", 2 * C), ("wproj", 2 * C),
    ("btok", 2), ("bproj", 2), ("wgate", 2 * E), ("temp", TRIPLES), ("gbias", E)])
CON, CON_W = _columns([
    ("ident", 128), ("before", TM), ("eye", N), ("qmask", HH), ("omask", HH), ("rank8", E),
    ("steps", SHT), ("tileno", RTILES)])


def build_program(nc, xT, params, consts, w_up, w_down, out, xbuf, ybuf):
    ctx = ExitStack()

    def sb(name, shape, dt=F32):
        return ctx.enter_context(nc.sbuf_tensor(name, shape, dt))

    def sem(name):
        return ctx.enter_context(nc.semaphore(name))

    with ctx:
        W = sb("W", [128, (E + 1) * WF])
        par = sb("par", [128, PAR_W])
        con = sb("con", [128, CON_W])
        h1 = sb("h1", [TM, TILES, C])
        logits = sb("logits", [TM, TILES, E])
        pos = sb("pos", [TM, 2, TILES], I32)
        wgt = sb("wgt", [TM, 2, TILES])
        tile_w = sb("tile_w", [1, RTILES], I32)
        ones = sb("ones", [TM, TM])
        phalf = sb("phalf", [TM, TILES * E])
        mhalf = sb("mhalf", [TM, TILES])
        zero = sb("zero", [128, C])

        arena_at = [(E - 3) * WF]

        def arena(parts, *shape):
            n = int(np.prod(shape))
            v = W[0:parts, arena_at[0]:arena_at[0] + n]
            arena_at[0] += n
            assert arena_at[0] <= E * WF
            if len(shape) == 1:
                return v
            names = [f"d{i}" for i in range(len(shape))]
            return v.rearrange(f"p ({' '.join(names)}) -> p {' '.join(names)}",
                               **{n_: s for n_, s in zip(names, shape)})

        xin = arena(128, KI, GT)
        hT = arena(HC, 2, G, 64)
        h0b = arena(HC, 2, GT)
        qblk = arena(RT, 2, G, ROWS)
        kT = arena(RT, 2, GT)
        vv = arena(128, 4, C)
        S = [arena(ROWS, 16, 64) for _ in range(2)]
        PT = [arena(128, 2, TRIPLES * ROWS) for _ in range(2)]
        oT = arena(RT, 2, GT)
        tmask = arena(ROWS, 2, 2, N)
        h1T = arena(HC, GTILES, 2, TM)
        smax = arena(ROWS, 2, 16)
        ssum = arena(ROWS, 2, 16)
        h1g = arena(TM, GTILES, C)
        stats = arena(TM, GTILES, 6)
        mv = arena(TM, GTILES, 2)
        veps = arena(TM, GTILES)
        rstd = arena(TM, GTILES)
        ntemp = arena(ROWS, TRIPLES)

        xt = sb("xt", [128, 2, C])
        xtT = sb("xtT", [HC, 2, 2, XT])
        sg = sb("sg", [128, I])
        up = sb("up", [128, I])
        hh = sb("hh", [128, I])
        hhT = sb("hhT", [128, IC, XT])
        yy = sb("yy", [128, 2, C])

        def routing(i, *shape):
            v = par[0:TM, i * TILES * E:i * TILES * E + int(np.prod(shape))]
            return v.rearrange("p (k e) -> p k e", k=shape[0]) if len(shape) == 2 else v

        assert 14 * TILES * E <= PAR["wgate"][0]
        FS, FB = 4, 6
        FQ = TILES // FB
        fin = W[0:TM, 0:FS * 3 * C].rearrange("p (s w n) -> p s w n", s=FS, w=3)
        fstats = sb("fstats", [TM, TILES, 6])
        fmv = sb("fmv", [TM, TILES, 2])
        fve = sb("fve", [TM, TILES])
        frs = sb("frs", [TM, TILES])

        bank = [ctx.enter_context(nc.psum_tensor(f"bank{i}", [128, 512], F32)) for i in range(8)]

        def P(name):
            a, b = PAR[name]
            return par[:, a:b]

        def K(name):
            a, b = CON[name]
            return con[:, a:b]

        wtok = P("wtok").rearrange("p (c n) -> p c n", c=KI)
        wq = P("wq").rearrange("p (c t n) -> p c t n", c=2, t=2)
        wk = P("wk").rearrange("p (c t n) -> p c t n", c=2, t=2)
        wv = P("wv").rearrange("p (c n) -> p c n", c=2)
        wproj = P("wproj").rearrange("p (t n) -> p t n", t=2)
        wgate = P("wgate").rearrange("p (c n) -> p c n", c=2)
        ident = K("ident")

        s_par = sem("params_in")
        s_xin = sem("group_in")
        s_w = [sem(f"expert_in{e}") for e in range(E + 1)]
        s_zero = sem("zeroed")
        s_zfill = sem("dispatch_zeroed")
        s_tok = sem("tok_done")
        s_hT = sem("hT_ready")
        s_h0b = sem("h0b_ready")
        s_qk = sem("qk_done")
        s_q = sem("q_ready")
        s_k = sem("k_ready")
        s_vd = sem("v_done")
        s_v = sem("v_ready")
        s_S = sem("scores_done")
        s_sm = sem("scores_masked")
        s_mx = sem("max_ready")
        s_sub = sem("max_subtracted")
        s_ex = sem("exp_ready")
        s_sr = sem("sums_inverted")
        s_pn = sem("probs_ready")
        s_T = sem("probsT_done")
        s_PT = sem("probsT_ready")
        s_O = sem("heads_done")
        s_oT = sem("heads_ready")
        s_pj = sem("proj_done")
        s_var = sem("var_ready")
        s_rstd = sem("rstd_ready")
        s_h1 = sem("h1_ready")
        s_h1o = sem("h1_out")
        s_h1k = sem("h1_kept")
        s_hTd = sem("h1T_done")
        s_h1T = sem("h1T_ready")
        s_lg = sem("logits_done")
        s_lgr = sem("logits_ready")
        s_ntemp = sem("temperature_mask")
        s_st = sem("stats_ready")
        s_ag = sem("mean_var_ready")
        s_su = sem("sums_ready")
        s_ext = sem("heads_partly_read")
        s_route = sem("routing_chain")
        s_ract = sem("routing_act")
        s_sq = sem("sqrt_ready")
        s_cnt = sem("counts_done")
        s_pos = sem("positions_ready")
        s_scat = sem("rows_dispatched")
        s_xl = [sem(f"x_in{i}") for i in range(2)]
        s_xd = sem("xT_done")
        s_xT = sem("xT_ready")
        s_ud = sem("up_done")
        s_sg = sem("silu_ready")
        s_ur2 = sem("up_clipped")
        s_h = sem("h_ready")
        s_hd = sem("hT_tile_done")
        s_hTt = sem("hT_tile_ready")
        s_yd = sem("y_done")
        s_y = sem("y_ready")
        s_yo = [sem(f"y_out{i}") for i in range(2)]
        s_f = [sem(f"chosen_rows_in{i}") for i in range(FS)]
        s_fs = [sem(f"shared_rows_in{i}") for i in range(FS)]
        s_fa = sem("rows_added")
        s_fst = sem("final_stats")
        s_fag = sem("final_mean_var")
        s_fv = sem("final_var")
        s_fr = sem("final_rstd")
        s_fn = sem("final_rows")
        s_fo = sem("output_stored")

        def wait_apart(eng, signal, count):
            count = count if isinstance(count, int) else eng.compute_val(count)
            eng.wait_ge(s_par, 32)
            eng.wait_ge(signal, count)

        block = ctx.enter_context(nc.Block())

        halves = [(h, h * 4) for h in range(2)]

        @block.sync
        def _(sp):
            def load_group(g):
                sp.dma_start(xin, xT[:, :, bass.ds(g * GT, GT)].rearrange("c p n -> p c n")).then_inc(s_xin, 16)

            def store_out(q):
                sp.wait_ge(s_fn, q + 1)
                sp.dma_start(out[q * FB * TM:(q + 1) * FB * TM, :].rearrange("(t p) n -> p t n", p=TM),
                             h1[:, q * FB:(q + 1) * FB, :]).then_inc(s_fo, 16)

            def load_expert(e):
                sp.dma_start(W[0:HC, e * WF:e * WF + UPF], w_up[e]).then_inc(s_w[e], 16)
                sp.dma_start(W[:, e * WF + UPF:(e + 1) * WF], w_down[e]).then_inc(s_w[e], 16)

            def store_h1(g):
                sp.wait_ge(s_h1, g * GTILES + GTILES)
                sp.dma_start(xbuf[bass.ds(g * GT, GT), :].rearrange("(t p) n -> p t n", p=TM),
                             h1g).then_inc(s_h1o, 16)
                sp.dma_start(h1[:, bass.ds(g * GTILES, GTILES), :], h1g).then_inc(s_h1k, 16)

            sp.dma_start(par[:, :], params).then_inc(s_par, 16)
            sp.dma_start(con[:, :], consts).then_inc(s_par, 16)
            load_group(0)
            sp.wait_ge(s_tok, 2)
            load_group(1)
            sp.wait_ge(s_zero, 1)
            sp.dma_start(xbuf[TOKENS:XROWS, :].rearrange("(t p) n -> p t n", p=128),
                         zero[:, :].rearrange("p (o n) -> p o n", o=1).to_broadcast([128, RTILES, C])
                         ).then_inc(s_zfill, 16)
            load_expert(E)
            for e in range(E - 3):
                load_expert(e)
            with sp.Fori(0, GROUPS - 2) as g:
                sp.wait_ge(s_tok, g * 2 + 4)
                load_group(g + 2)
                store_h1(g)
            store_h1(GROUPS - 2)
            store_h1(GROUPS - 1)
            sp.wait_ge(s_lgr, GROUPS)
            sp.wait_ge(s_pj, GROUPS * GTILES)
            sp.wait_ge(s_h1, GROUPS * GTILES)
            sp.wait_ge(s_h1o, 16 * GROUPS)
            sp.wait_ge(s_h1k, 16 * GROUPS)
            for e in range(E - 3, E):
                load_expert(e)

            def load_x(i, b):
                sp.dma_start(xt[:, b, :], xbuf[bass.ds(i * XT, XT), :]).then_inc(s_xl[b], 16)

            def store_y(i, b):
                sp.wait_ge(s_y, i + 1)
                sp.dma_start(ybuf[bass.ds(i * XT, XT), :], yy[:, b, :]).then_inc(s_yo[b], 16)

            def step(i, b, routed=False):
                sp.wait_ge(s_xd, i + 1)
                load_x(i + 2, b)
                store_y(i - 1, 1 - b)

            sp.wait_ge(s_h1o, 16 * GROUPS)
            load_x(0, 0)
            load_x(1, 1)
            sp.wait_ge(s_xd, 1)
            load_x(2, 0)
            with sp.Fori(0, 7) as it:
                step(it * 2 + 1, 1)
                step(it * 2 + 2, 0)
            step(15, 1)
            sp.wait_ge(s_scat, 16 * 2 * TILES)
            step(16, 0)
            with sp.Fori(0, (ALLT - 2 - 17) // 2) as it:
                step(it * 2 + 17, 1)
                step(it * 2 + 18, 0)
            for i in range(ALLT - 2, ALLT + 1):
                store_y(i - 1, (i - 1) % 2)

            for b in range(2):
                sp.wait_ge(s_yo[b], 16 * ((ALLT + 1 - b) // 2))
            for q in range(FQ):
                for k in range(q * FB, (q + 1) * FB):
                    if k >= FS:
                        sp.wait_ge(s_fa, 3 * (k - FS) + 3)
                    sp.dma_start(fin[:, k % FS, 0, :], ybuf[k * TM:(k + 1) * TM, :]).then_inc(s_fs[k % FS], 16)
                if q > 0:
                    store_out(q - 1)
            store_out(FQ - 1)
            sp.wait_ge(s_fo, 16 * FQ)

        @block.tensor
        def _(pe):
            def embed(g):
                pe.wait_ge(s_xin, g * 16 + 16)
                if not (isinstance(g, int) and g == 0):
                    pe.wait_ge(s_v, g * 2)
                for mt in range(2):
                    for c in range(KI):
                        m = pe.matmul(bank[mt][0:HC, 0:GT], wtok[:, c, mt * HC:(mt + 1) * HC], xin[:, c, :],
                                      start=(c == 0), stop=(c == KI - 1))
                    m.then_inc(s_tok, 1)

            def qk(g):
                pe.wait_ge(s_hT, g * 2 + 2)
                for x, (w, b0) in enumerate(((wq, 0), (wk, 6))):
                    for tp in range(2):
                        for c in range(2):
                            m = pe.matmul(bank[b0 + tp][0:RT, 0:GT], w[0:HC, c, tp, :], hT[:, c, :, 0:N],
                                          start=(c == 0), stop=(c == 1))
                        m.then_inc(s_qk, 1)

            def values(g):
                pe.wait_ge(s_q, g * 2 + 2)
                for half in range(2):
                    for pair in range(2):
                        at = half * 4 + pair * 2
                        for c in range(2):
                            st = hT[:, c, at:at + 2, :].rearrange("p r m -> p (r m)")
                            m = pe.matmul(bank[half][:, pair * C:(pair + 1) * C], st, wv[0:HC, c, :],
                                          start=(c == 0), stop=(c == 1))
                    m.then_inc(s_vd, 1)

            def scores(g, h):
                if h == 0:
                    pe.wait_ge(s_q, g * 2 + 2)
                    pe.wait_ge(s_k, g * 2 + 2)
                elif not (isinstance(g, int) and g == 0):
                    pe.wait_ge(s_h1, g * GTILES)
                for tp in range(2):
                    for b in range(4):
                        for j in range(2):
                            im, at = h * 4 + b, (tp * 4 + b) * N
                            m = pe.matmul(bank[4 + 2 * h + j][0:ROWS, at:at + N],
                                          qblk[64 * j:64 * j + 48, tp, im, :],
                                          kT[64 * j:64 * j + 48, tp, im * N:(im + 1) * N], start=True, stop=True)
                m.then_inc(s_S, 1)

            def probsT(g, h):
                pe.wait_ge(s_pn, g * 2 + h + 1)
                for pair in range(2):
                    for j in range(2):
                        for tp in range(2):
                            at = ((j * 2 + tp) * 2 + pair) * 2
                            src = S[h][:, at:at + 2, :].rearrange("p r m -> p (r m)")
                            m = pe.transpose(bank[2 + pair][:, (tp * 2 + j) * ROWS:(tp * 2 + j + 1) * ROWS],
                                             src, ident[0:ROWS, 0:ROWS])
                    m.then_inc(s_T, 1)

            def heads(g, h):
                pe.wait_ge(s_v, g * 2 + 2)
                if h == 1:
                    pe.wait_ge(s_oT, g * 4 + 2)
                else:
                    pe.wait_ge(s_sm, g * 2 + 1)
                wait_apart(pe, s_PT, g * 4 + 2 * h + 2)
                for r in range(2):
                    for tp in range(2):
                        for pair in range(2):
                            for j in range(2):
                                t = 2 * tp + j
                                at = (tp * 2 + pair) * ROWS
                                wide = 64 if j == 0 else 48
                                m = pe.matmul(bank[4 + r][64 * j:64 * j + wide, at:at + ROWS],
                                              vv[64 * r:64 * r + N, h * 2 + pair, t * 48:t * 48 + wide],
                                              PT[h][64 * r:64 * r + N, pair, t * ROWS:(t + 1) * ROWS],
                                              start=True, stop=True)
                    m.then_inc(s_O, 1)

            def proj(g):
                pe.wait_ge(s_oT, g * 4 + 4)
                pe.wait_ge(s_h0b, g + 1)
                for t in range(GTILES):
                    o = bank[6 + t // 2][0:TM, (t % 2) * C:(t % 2 + 1) * C]
                    for tp in range(2):
                        pe.matmul(o, oT[:, tp, t * TM:(t + 1) * TM], wproj[0:RT, tp, :],
                                  start=(tp == 0), stop=False, skip_group_check=True)
                    for c in range(2):
                        m = pe.matmul(o[:, c * HC:(c + 1) * HC], h0b[:, c, t * TM:(t + 1) * TM],
                                      ident[0:HC, 0:HC], start=False, stop=(c == 1), skip_group_check=True)
                    m.then_inc(s_pj, 1)

            def router_T(g):
                pe.wait_ge(s_h1, g * GTILES + GTILES)
                for t in range(GTILES):
                    for c in range(2):
                        at = ((t % 2) * 2 + c) * TM
                        m = pe.transpose(bank[2 + t // 2][0:HC, at:at + TM],
                                         h1g[:, t, c * HC:(c + 1) * HC], ident[0:TM, 0:TM])
                    if t > 0:
                        m.then_inc(s_hTd, 1)

            def router(g):
                pe.wait_ge(s_h1T, g * 2 + 2)
                for t in range(GTILES):
                    for c in range(2):
                        m = pe.matmul(bank[3][0:TM, 400 + t * E:400 + (t + 1) * E], h1T[:, t, c, :], wgate[0:HC, c, :],
                                      start=(c == 0), stop=(c == 1))
                m.then_inc(s_lg, 1)

            pe.wait_ge(s_par, 32)
            pe.wait_ge(s_zero, 1)
            embed(0)
            qk(0)
            values(0)

            def group(g, first=False, last=False):
                scores(g, 0)
                scores(g, 1)
                if not first:
                    router_T(g - 1)
                if not last:
                    embed(g + 1)
                if not first:
                    router(g - 1)
                    pe.wait_ge(s_lgr, g)
                probsT(g, 0)
                heads(g, 0)
                if not last:
                    pe.wait_ge(s_sm, g * 2 + 2)
                    qk(g + 1)
                probsT(g, 1)
                heads(g, 1)
                if not last:
                    values(g + 1)
                    pe.wait_ge(s_k, g * 2 + 4)
                proj(g)

            group(0, first=True)
            with pe.Fori(1, GROUPS - 1) as g:
                group(g)
            group(GROUPS - 1, last=True)
            router_T(GROUPS - 1)
            router(GROUPS - 1)

            def counts():
                pe.wait_ge(s_route, ROUTE_CHOICES)
                rows = routing(13, TILES * E)
                pe.matmul(bank[0][0:TM, 0:TILES * E], K("before")[0:TM], rows, start=True, stop=True)
                pe.matmul(bank[1][0:TM, 0:TILES * E], ones[:, :], rows, start=True, stop=True).then_inc(s_cnt, 1)

            def X(i, b):
                pe.wait_ge(s_xl[b], (i - b) * 8 + 16)
                for c in range(2):
                    m = pe.transpose(bank[7][0:HC, c * XT:(c + 1) * XT], xt[:, b, c * HC:(c + 1) * HC], ident)
                m.then_inc(s_xd, 1)

            def U(i, b, off):
                pe.wait_ge(s_xT, i + 1)
                for k in range(2):
                    if not (isinstance(i, int) and i == 0):
                        pe.wait_ge(s_sg if k == 0 else s_ur2, i)
                    for n in range(2):
                        for c in range(2):
                            m = pe.matmul(bank[2 * k + n][:, 0:I // 2], xtT[:, b, c, :],
                                          W[0:HC, bass.ds(off + (k * 2 + c) * I + n * (I // 2), I // 2)],
                                          start=(c == 0), stop=(c == 1))
                    m.then_inc(s_ud, 1)

            def H(i):
                pe.wait_ge(s_h, i + 1)
                for q in range(2):
                    for c in range(3):
                        ic = q * 3 + c
                        m = pe.transpose(bank[4 + q][:, c * XT:(c + 1) * XT], hh[:, ic * 128:(ic + 1) * 128], ident)
                    m.then_inc(s_hd, 1)

            def D(i, off):
                pe.wait_ge(s_hTt, i * 2 + 2)
                if not (isinstance(i, int) and i == 0):
                    pe.wait_ge(s_y, i)
                for ic in range(IC):
                    m = pe.matmul(bank[6][:, 0:C], hhT[:, ic, :], W[:, bass.ds(off + UPF + ic * C, C)],
                                  start=(ic == 0), stop=(ic == IC - 1))
                m.then_inc(s_yd, 1)

            def expert_of(i):
                return pe.value_load(tile_w[0:1, bass.ds(i - SHT, 1)], min_val=0, max_val=(E - 1) * WF)

            def step(i, b, prev, cur, last=False):
                H(i - 1)
                U(i, b, cur)
                D(i - 1, prev)
                if not last:
                    X(i + 1, 1 - b)

            shared = E * WF
            pe.wait_ge(s_w[E], 32)
            pe.wait_ge(s_h1, GROUPS * GTILES)
            counts()
            X(0, 0)
            pe.wait_ge(s_pos, 1)
            U(0, 0, shared)
            X(1, 1)
            with pe.Fori(0, 8) as it:
                step(it * 2 + 1, 1, shared, shared)
                step(it * 2 + 2, 0, shared, shared)
            step(17, 1, shared, shared)
            for e in range(E):
                pe.wait_ge(s_w[e], 32)
            pe.wait_ge(s_pos, 1)
            step(18, 0, shared, expert_of(18))
            with pe.Fori(0, (ALLT - 19 - 2) // 2) as it:
                step(it * 2 + 19, 1, expert_of(it * 2 + 18), expert_of(it * 2 + 19))
                step(it * 2 + 20, 0, expert_of(it * 2 + 19), expert_of(it * 2 + 20))
            step(ALLT - 2, 1, expert_of(ALLT - 3), expert_of(ALLT - 2))
            step(ALLT - 1, 0, expert_of(ALLT - 2), expert_of(ALLT - 1), last=True)
            H(ALLT - 1)
            D(ALLT - 1, expert_of(ALLT - 1))

        @block.scalar
        def _(act):
            def hT_out(g):
                if not (isinstance(g, int) and g == 0):
                    act.wait_ge(s_h0b, g)
                for mt in range(2):
                    act.wait_ge(s_tok, g * 2 + mt + 1)
                    nc.scalar.activation(hT[:, mt, :, 0:N], bank[mt][0:HC, 0:GT].rearrange("p (b n) -> p b n", b=G), ACT.Identity,
                                         bias=P("btok")[0:HC, mt:mt + 1]).then_inc(s_hT, 1)

            def k_out(g):
                for tp in range(2):
                    act.wait_ge(s_qk, g * 4 + 3 + tp)
                    nc.scalar.copy(kT[:, tp, :], bank[6 + tp][0:RT, 0:GT]).then_inc(s_k, 1)

            def v_out(g):
                for half in range(2):
                    act.wait_ge(s_vd, g * 2 + half + 1)
                    nc.scalar.copy(vv[:, half * 2:half * 2 + 2, :],
                                   bank[half][:, 0:2 * C].rearrange("p (a n) -> p a n", a=2)).then_inc(s_v, 1)

            def exps(g, h):
                act.wait_ge(s_sub, g * 2 + h + 1)
                nc.scalar.activation(S[h][:, :, 0:N], S[h][:, :, 0:N], ACT.Exp).then_inc(s_ex, 1)

            def probsT_out(g, h):
                for pair in range(2):
                    act.wait_ge(s_T, g * 4 + h * 2 + pair + 1)
                    nc.scalar.copy(PT[h][:, pair, :], bank[2 + pair][:, 0:TRIPLES * ROWS]).then_inc(s_PT, 1)

            def h1T_out(g):
                act.wait_ge(s_hTd, g * 2 + 1)
                nc.scalar.copy(h1T[:, 0:2, :, :], bank[2][0:HC, 0:4 * TM]
                               .rearrange("p (t c n) -> p t c n", t=2, c=2)).then_inc(s_h1T, 1)
                act.wait_ge(s_hTd, g * 2 + 2)
                nc.scalar.copy(h1T[:, 2, :, :], bank[3][0:HC, 0:2 * TM]
                               .rearrange("p (c n) -> p c n", c=2)).then_inc(s_h1T, 1)

            def logits_out(g):
                act.wait_ge(s_lg, g + 1)
                nc.scalar.copy(logits[:, bass.ds(g * GTILES, GTILES), :], bank[3][0:TM, 400:400 + GTILES * E]
                               .rearrange("p (t e) -> p t e", t=GTILES)).then_inc(s_lgr, 1)

            def group(g, first=False, last=False):
                exps(g, 0)
                if not first:
                    h1T_out(g - 1)
                if not last:
                    hT_out(g + 1)
                if not first:
                    logits_out(g - 1)
                exps(g, 1)
                probsT_out(g, 0)
                if not last:
                    k_out(g + 1)
                probsT_out(g, 1)
                if not last:
                    v_out(g + 1)

            act.wait_ge(s_par, 32)
            act.wait_ge(s_zero, 1)
            hT_out(0)
            k_out(0)
            v_out(0)
            group(0, first=True)
            with act.Fori(1, GROUPS - 1) as g:
                group(g)
            group(GROUPS - 1, last=True)
            h1T_out(GROUPS - 1)
            logits_out(GROUPS - 1)

            act.wait_ge(s_route, 1)
            nc.scalar.activation(routing(1, TILES * E), routing(0, TILES * E), ACT.Exp, scale=-1.0).then_inc(s_ract, 1)
            act.wait_ge(s_route, 2)
            nc.scalar.activation(routing(3, TILES * E), routing(2, TILES * E), ACT.Ln).then_inc(s_ract, 1)

            def x_out(i, b):
                act.wait_ge(s_xd, i + 1)
                nc.scalar.copy(xtT[:, b, :, :], bank[7][0:HC, 0:2 * XT].rearrange("p (c n) -> p c n", c=2)).then_inc(s_xT, 1)

            def silu(i):
                act.wait_ge(s_ud, i * 2 + 1)
                if not (isinstance(i, int) and i == 0):
                    act.wait_ge(s_h, i)
                for n in range(2):
                    a = nc.scalar.activation(sg[:, n * (I // 2):(n + 1) * (I // 2)], bank[n][:, 0:I // 2], ACT.Silu)
                a.then_inc(s_sg, 1)

            def hT_tile_out(i):
                for q in range(2):
                    act.wait_ge(s_hd, i * 2 + q + 1)
                    nc.scalar.copy(hhT[:, q * 3:q * 3 + 3, :], bank[4 + q][:, 0:3 * XT]
                                   .rearrange("p (c n) -> p c n", c=3)).then_inc(s_hTt, 1)

            def step(i, b, last=False):
                hT_tile_out(i - 1)
                silu(i)
                if not last:
                    x_out(i + 1, 1 - b)

            x_out(0, 0)
            silu(0)
            x_out(1, 1)
            with act.Fori(0, (ALLT - 3) // 2) as it:
                step(it * 2 + 1, 1)
                step(it * 2 + 2, 0)
            step(ALLT - 2, 1)
            step(ALLT - 1, 0, last=True)
            hT_tile_out(ALLT - 1)

        @block.vector
        def _(dve):
            V = nc.vector

            def q_out(g):
                for tp in range(2):
                    dve.wait_ge(s_qk, g * 4 + 1 + tp)
                    src = bank[tp][0:RT, 0:GT].rearrange("p (b o n) -> p b o n", b=G, o=1).to_broadcast([RT, G, HH, N])
                    msk = K("qmask")[0:RT].rearrange("p (o h u) -> p o h u", o=1, u=1).to_broadcast([RT, G, HH, N])
                    V.tensor_tensor(qblk[:, tp].rearrange("p b (h n) -> p b h n", h=HH), src, msk,
                                    ALU.mult).then_inc(s_q, 1)

            def mask_max(g, h):
                dve.wait_ge(s_S, g * 2 + h + 1)
                for j in range(2):
                    m = V.tensor_tensor(S[h][:, j * 8:j * 8 + 8, 0:N].rearrange("p (t b) m -> p t b m", t=2),
                                        bank[4 + 2 * h + j][0:ROWS, 0:8 * N].rearrange("p (t b m) -> p t b m", t=2, b=4),
                                        tmask[:, j].rearrange("p t (o m) -> p t o m", o=1)
                                        .to_broadcast([ROWS, 2, 4, N]), ALU.mult)
                m.then_inc(s_sm, 1)
                dve.wait_ge(s_sm, g * 2 + h + 1)
                V.tensor_reduce(smax[:, h, :], S[h][:, :, 0:N],
                                AX.X, ALU.max, negate=True).then_inc(s_mx, 1)

            def sums(g, h):
                dve.wait_ge(s_ex, g * 2 + h + 1)
                V.tensor_reduce(ssum[:, h, :], S[h][:, :, 0:N],
                                AX.X, ALU.add).then_inc(s_su, 1)
                dve.wait_ge(s_su, g * 2 + h + 1)
                V.reciprocal(ssum[:, h, :], ssum[:, h, :]).then_inc(s_sr, 1)

            def heads_out(g, h):
                for r in range(2):
                    dve.wait_ge(s_O, g * 4 + h * 2 + r + 1)
                for k in range(HH):
                    for r in range(2):
                        src = bank[4 + r][0:RT, 0:4 * ROWS].rearrange("p (t a x) -> p t a x", t=2, a=2)[:, :, :, k * N:(k + 1) * N]
                        at = (h * 4 + r * 2) * N
                        dst = oT[:, :, at:at + 2 * N].rearrange("p t (a n) -> p t a n", a=2)
                        msk = K("omask")[0:RT, k:k + 1]
                        if k == 0:
                            V.tensor_scalar(dst, src, msk, None, ALU.mult).then_inc(s_ext, 1)
                        else:
                            dve.wait_ge(s_ext, g * 8 + h * 4 + (k - 1) * 2 + r + 1)
                            V.scalar_tensor_tensor(out=dst, in0=src, scalar=msk, in1=dst, op0=ALU.mult,
                                                   op1=ALU.add).then_inc(s_ext if k < HH - 1 else s_oT, 1)

            def norm(g):
                for t in range(GTILES):
                    dve.wait_ge(s_pj, g * GTILES + min(2 * (t // 2) + 2, GTILES))
                    V.bn_stats(stats[:, t, :], bank[6 + t // 2][0:TM, (t % 2) * C:(t % 2 + 1) * C]).then_inc(s_st, 1)
                for t in range(GTILES):
                    wait_apart(dve, s_st, g * GTILES + t + 1)
                    V.bn_aggr(mv[:, t, :], stats[:, t, :]).then_inc(s_ag, 1)
                dve.wait_ge(s_ag, g * GTILES + GTILES)
                V.tensor_scalar(veps, mv[:, :, 1], EPS, None, ALU.add).then_inc(s_var, 1)
                dve.wait_ge(s_rstd, g + 1)
                if not (isinstance(g, int) and g == 0):
                    dve.wait_ge(s_h1o, g * 16)
                    dve.wait_ge(s_h1k, g * 16)
                    dve.wait_ge(s_hTd, g * 2)
                for t in range(GTILES):
                    V.tensor_scalar(h1g[:, t, :], bank[6 + t // 2][0:TM, (t % 2) * C:(t % 2 + 1) * C],
                                    mv[:, t, 0:1], rstd[:, t:t + 1], ALU.subtract, ALU.mult).then_inc(s_h1, 1)

            def group(g, last=False):
                mask_max(g, 0)
                mask_max(g, 1)
                sums(g, 0)
                sums(g, 1)
                heads_out(g, 0)
                if not last:
                    q_out(g + 1)
                heads_out(g, 1)
                norm(g)

            dve.wait_ge(s_par, 32)
            V.tensor_scalar(ntemp, P("temp")[0:ROWS], -1.0, None, ALU.mult).then_inc(s_ntemp, 1)
            dve.wait_ge(s_ntemp, 1)
            for tp in range(2):
                for j in range(2):
                    t = 2 * tp + j
                    V.tensor_scalar(tmask[:, j, tp, :], K("eye")[0:ROWS], ntemp[:, t:t + 1], 1.0,
                                    ALU.mult, ALU.add).then_inc(s_ntemp, 1)
            dve.wait_ge(s_ntemp, 5)
            dve.wait_ge(s_zero, 1)
            q_out(0)
            group(0)
            with dve.Fori(1, GROUPS - 1) as g:
                group(g)
            group(GROUPS - 1, last=True)

            n = [0]

            def link(ins):
                n[0] += 1
                ins.then_inc(s_route, 1)
                dve.wait_ge(s_route, n[0])

            TE = TILES * E
            flat, bias = (lambda i: routing(i, TE)), P("gbias")[0:TM]
            cube = lambda i: routing(i, TILES, E)
            over_k = lambda v: v.rearrange("p (o e) -> p o e", o=1).to_broadcast([TM, TILES, E])
            over_e = lambda v: v.rearrange("p (k o) -> p k o", o=1).to_broadcast([TM, TILES, E])
            L = logits[:, :, :].rearrange("p k e -> p (k e)")
            dve.wait_ge(s_lgr, GROUPS)
            dve.wait_ge(s_pj, GROUPS * GTILES)
            dve.wait_ge(s_lg, GROUPS)
            link(V.scalar_tensor_tensor(out=flat(0), in0=L, scalar=-1.0, in1=L, op0=ALU.mult, op1=ALU.max))
            dve.wait_ge(s_ract, 1)
            link(V.tensor_scalar(flat(2), flat(1), 1.0, None, ALU.add))
            link(V.tensor_scalar(flat(4), flat(2), -1.0, None, ALU.add))
            link(V.tensor_scalar(flat(5), flat(4), 0.0, None, ALU.is_equal))
            link(V.tensor_tensor(flat(4), flat(4), flat(5), ALU.add))
            link(V.reciprocal(flat(4), flat(4)))
            link(V.tensor_tensor(flat(4), flat(4), flat(1), ALU.mult))
            link(V.tensor_tensor(flat(5), flat(5), flat(1), ALU.mult))
            dve.wait_ge(s_ract, 2)
            link(V.tensor_tensor(flat(4), flat(4), flat(3), ALU.mult))
            link(V.tensor_tensor(flat(4), flat(4), flat(5), ALU.add))
            link(V.scalar_tensor_tensor(out=flat(6), in0=L, scalar=0.0, in1=flat(4), op0=ALU.max, op1=ALU.add))
            assert n[0] == ROUTE_SOFTPLUS
            dve.wait_ge(s_sq, 1)
            link(V.tensor_tensor(cube(8), cube(7), over_k(bias), ALU.add))
            for c, chosen in ((0, 9), (1, 10)):
                top, rank = flat(11)[:, 0:TILES], flat(11)[:, TILES:2 * TILES]
                link(V.tensor_reduce(top, cube(8), AX.X, ALU.max))
                link(V.tensor_tensor(cube(12), cube(8), over_e(top), ALU.is_equal))
                link(V.tensor_tensor(cube(12), cube(12), over_k(K("rank8")[0:TM]), ALU.mult))
                link(V.tensor_reduce(rank, cube(12), AX.X, ALU.max))
                link(V.tensor_tensor(cube(chosen), cube(12), over_e(rank), ALU.is_equal))
                if c == 0:
                    link(V.scalar_tensor_tensor(out=flat(8), in0=flat(chosen), scalar=-BIG, in1=flat(8),
                                                op0=ALU.mult, op1=ALU.add))
            link(V.tensor_tensor(flat(13), flat(9), flat(10), ALU.add))
            assert n[0] == ROUTE_CHOICES
            for c, chosen in ((0, 9), (1, 10)):
                link(V.tensor_tensor(flat(12), flat(chosen), flat(7), ALU.mult))
                link(V.tensor_reduce(wgt[:, c, :], cube(12), AX.X, ALU.add))
            link(V.tensor_tensor(flat(11)[:, 0:TILES], wgt[:, 0, :], wgt[:, 1, :], ALU.add))
            link(V.tensor_scalar(flat(11)[:, 0:TILES], flat(11)[:, 0:TILES], 1e-6, None, ALU.max))
            link(V.reciprocal(flat(11)[:, 0:TILES], flat(11)[:, 0:TILES]))
            for c in range(2):
                link(V.tensor_tensor(wgt[:, c, :], wgt[:, c, :], flat(11)[:, 0:TILES], ALU.mult))
            dve.wait_ge(s_cnt, 1)
            link(V.tensor_copy(flat(0), bank[1][0:TM, 0:TE]))
            a, b, d = 0, 1, 1
            while d < TILES:
                V.tensor_copy(cube(b)[:, 0:d, :], cube(a)[:, 0:d, :])
                link(V.tensor_tensor(cube(b)[:, d:, :], cube(a)[:, d:, :], cube(a)[:, 0:TILES - d, :], ALU.add))
                a, b, d = b, (2 if b == 1 else 1), d * 2
            incl = a
            count = cube(incl)[:, TILES - 1, :]
            link(V.tensor_tensor(flat(3), flat(incl), flat(0), ALU.subtract))
            link(V.tensor_tensor(flat(3), flat(3), bank[0][0:TM, 0:TE], ALU.add))
            ge = routing(4, E, SHT)
            link(V.tensor_tensor(ge, count.rearrange("p (e o) -> p e o", o=1).to_broadcast([TM, E, SHT]),
                                 K("steps")[0:TM].rearrange("p (o s) -> p o s", o=1).to_broadcast([TM, E, SHT]), ALU.is_gt))
            ends, ends2 = flat(11)[:, 0:E], flat(11)[:, E:2 * E]
            nt = flat(11)[:, 2 * E:3 * E]
            link(V.tensor_reduce(nt, ge, AX.X, ALU.add))
            link(V.tensor_copy(ends, nt))
            for d in (1, 2, 4):
                V.tensor_copy(ends2[:, 0:d], ends[:, 0:d])
                link(V.tensor_tensor(ends2[:, d:], ends[:, d:], ends[:, 0:E - d], ALU.add))
                ends, ends2 = ends2, ends
            base = flat(11)[:, 3 * E:4 * E]
            link(V.tensor_tensor(base, ends, nt, ALU.subtract))
            link(V.tensor_scalar(base, base, float(XT), float(TOKENS), ALU.mult, ALU.add))
            link(V.tensor_tensor(cube(3), cube(3), over_k(base), ALU.add))
            for c, chosen in ((0, 9), (1, 10)):
                link(V.tensor_tensor(flat(12), flat(chosen), flat(3), ALU.mult))
                link(V.tensor_reduce(flat(11)[:, 4 * E:4 * E + TILES], cube(12), AX.X, ALU.add))
                link(V.tensor_copy(pos[:, c, :], flat(11)[:, 4 * E:4 * E + TILES]))
            own = routing(4, RTILES, E)[0:1]
            link(V.tensor_tensor(own, ends[0:1].rearrange("p (o e) -> p o e", o=1).to_broadcast([1, RTILES, E]),
                                 K("tileno")[0:1].rearrange("p (t o) -> p t o", o=1).to_broadcast([1, RTILES, E]), ALU.is_le))
            tw = flat(12)[0:1, 0:RTILES]
            link(V.tensor_reduce(tw, own, AX.X, ALU.add))
            link(V.tensor_scalar(tw, tw, float(E - 1), float(WF), ALU.min, ALU.mult))
            V.tensor_copy(tile_w[:, :], tw).then_inc(s_pos, 1)

            def up_h(i):
                dve.wait_ge(s_ud, i * 2 + 2)
                for k in range(2):
                    m = V.tensor_scalar(up[:, k * (I // 2):(k + 1) * (I // 2)], bank[2 + k][:, 0:I // 2], LIMIT, -LIMIT,
                                        ALU.min, ALU.max)
                m.then_inc(s_ur2, 1)
                dve.wait_ge(s_ur2, i + 1)
                dve.wait_ge(s_sg, i + 1)
                if not (isinstance(i, int) and i == 0):
                    dve.wait_ge(s_hd, i * 2)
                V.scalar_tensor_tensor(out=hh[:, :], in0=sg[:, :], scalar=SILU_LIMIT, in1=up[:, :], op0=ALU.min,
                                       op1=ALU.mult).then_inc(s_h, 1)

            def y_out(i, b, reused=True):
                dve.wait_ge(s_yd, i + 1)
                if reused:
                    dve.wait_ge(s_yo[b], (i - b) * 8)
                V.tensor_copy(yy[:, b, :], bank[6][:, 0:C]).then_inc(s_y, 1)

            up_h(0)
            up_h(1)
            y_out(0, 0, reused=False)
            up_h(2)
            y_out(1, 1, reused=False)
            with dve.Fori(0, (ALLT - 3) // 2) as it:
                up_h(it * 2 + 3)
                y_out(it * 2 + 2, 0)
                up_h(it * 2 + 4)
                y_out(it * 2 + 3, 1)
            y_out(ALLT - 1, 0)

            def final_norm(q):
                dve.wait_ge(s_fr, q + 1)
                for k in range(q * FB, (q + 1) * FB):
                    m = V.tensor_scalar(h1[:, k, :], h1[:, k, :], fmv[:, k, 0:1], frs[:, k:k + 1], ALU.subtract, ALU.mult)
                m.then_inc(s_fn, 1)

            for q in range(FQ):
                for k in range(q * FB, (q + 1) * FB):
                    f, acc = k % FS, h1[:, k, :]
                    dve.wait_ge(s_fs[f], 16 * (k // FS + 1))
                    dve.wait_ge(s_f[f], 32 * (k // FS + 1))
                    if k == 0:
                        dve.wait_ge(s_h1k, 16 * GROUPS)
                    V.tensor_tensor(acc, acc, fin[:, f, 0, :], ALU.add).then_inc(s_fa, 1)
                    for c in range(2):
                        dve.wait_ge(s_fa, 3 * k + c + 1)
                        V.scalar_tensor_tensor(out=acc, in0=fin[:, f, 1 + c, :], scalar=wgt[:, c, k:k + 1], in1=acc,
                                               op0=ALU.mult, op1=ALU.add).then_inc(s_fa, 1)
                    dve.wait_ge(s_fa, 3 * k + 3)
                    V.bn_stats(fstats[:, k, :], acc).then_inc(s_fst, 1)
                    dve.wait_ge(s_fst, k + 1)
                    V.bn_aggr(fmv[:, k, :], fstats[:, k, :]).then_inc(s_fag, 1)
                dve.wait_ge(s_fag, (q + 1) * FB)
                V.tensor_scalar(fve[:, q * FB:(q + 1) * FB], fmv[:, q * FB:(q + 1) * FB, 1], EPS, None,
                                ALU.add).then_inc(s_fv, 1)
                if q > 0:
                    final_norm(q - 1)
            final_norm(FQ - 1)

        @block.gpsimd
        def _(pool):
            PO = nc.gpsimd
            for v, x in ((zero[:, :], 0.0), (ones[:, :], 1.0), (phalf[:, :], 0.5), (mhalf[:, :], -0.5),
                         (hT[:, :, :, N:64], 0.0), (S[0][:, :, N:64], 0.0), (S[1][:, :, N:64], 0.0)):
                m = PO.memset(v, x)
            m.then_inc(s_zero, 1)
            pool.wait_ge(s_zero, 1)
            pool.wait_ge(s_par, 32)

            def h0b_out(g):
                if not (isinstance(g, int) and g == 0):
                    pool.wait_ge(s_pj, g * GTILES)
                wait_apart(pool, s_hT, g * 2 + 2)
                for mt in range(2):
                    for half in range(2):
                        m = PO.tensor_scalar(
                            h0b[:, mt, half * 4 * N:(half + 1) * 4 * N].rearrange("p (r a n) -> p r a n", r=2, a=2),
                            hT[:, mt, half * 4:half * 4 + 4, 0:N].rearrange("p (a r) n -> p r a n", a=2),
                            P("bproj")[0:HC, mt:mt + 1], None, ALU.add)
                m.then_inc(s_h0b, 1)

            def per_segment(h, v, wait, op, done, g):
                pool.wait_ge(wait, g * 2 + h + 1)
                s = S[h][:, :, 0:N]
                PO.tensor_tensor(s, s, v[:, h, :].rearrange("p (s o) -> p s o", o=1).to_broadcast([ROWS, 16, N]),
                                 op).then_inc(done, 1)

            def group(g, last=False):
                for h in range(2):
                    per_segment(h, smax, s_mx, ALU.add, s_sub, g)
                for h in range(2):
                    per_segment(h, ssum, s_sr, ALU.mult, s_pn, g)
                pool.wait_ge(s_var, g + 1)
                PO.tensor_tensor(rstd, veps, mhalf[:, 0:GTILES], ALU.pow).then_inc(s_rstd, 1)
                if not last:
                    h0b_out(g + 1)

            h0b_out(0)
            with pool.Fori(0, GROUPS - 1) as g:
                group(g)
            group(GROUPS - 1, last=True)

            pool.wait_ge(s_route, ROUTE_SOFTPLUS)
            PO.tensor_tensor(routing(7, TILES * E), routing(6, TILES * E), phalf[:, :], ALU.pow).then_inc(s_sq, 1)
            pool.wait_ge(s_pos, 1)
            pool.wait_ge(s_zfill, 16)
            pool.wait_ge(s_h1k, 16 * GROUPS)
            for k in range(TILES):
                for c in range(2):
                    PO.indirect_dma_start(xbuf[:, :], bass.IndirectOffsetOnAxis(ap=pos[:, c, k:k + 1], axis=0),
                                          h1[:, k, :], None).then_inc(s_scat, 16)
            def final_rstd(q):
                pool.wait_ge(s_fv, q + 1)
                PO.tensor_tensor(frs[:, q * FB:(q + 1) * FB], fve[:, q * FB:(q + 1) * FB], mhalf[:, 0:FB],
                                 ALU.pow).then_inc(s_fr, 1)

            for b in range(2):
                pool.wait_ge(s_yo[b], 16 * ((ALLT + 1 - b) // 2))
            for q in range(FQ):
                for k in range(q * FB, (q + 1) * FB):
                    if k >= FS:
                        pool.wait_ge(s_fa, 3 * (k - FS) + 3)
                    for c in range(2):
                        PO.indirect_dma_start(fin[:, k % FS, 1 + c, :], None, ybuf[:, :],
                                              bass.IndirectOffsetOnAxis(ap=pos[:, c, k:k + 1], axis=0)
                                              ).then_inc(s_f[k % FS], 16)
                if q > 0:
                    final_rstd(q - 1)
            final_rstd(FQ - 1)


def _pack(columns, width, rows, fields):
    out = np.zeros((rows, width), np.float32)
    for name, v in fields.items():
        a, b = columns[name]
        out[:v.shape[0], a:b] = v.reshape(v.shape[0], b - a)
    return out


def _triples(w):
    w = w.reshape(*w.shape[:-1], 2, 2, HH * HD)
    out = np.zeros((*w.shape[:-3], 2, RT), np.float32)
    out[..., 0:48] = w[..., 0, :]
    out[..., 64:112] = w[..., 1, :]
    return out


def _chunks(w, p):
    return np.moveaxis(w.reshape(-1, p, *w.shape[1:]), 0, 1)


def kernel(x, L0_tok_W, L0_tok_b, L0_attn_w_qkv, L0_attn_w_proj, L0_attn_b_proj, L0_attn_temperature,
           L0_ffn_input_ids, L0_ffn_gate_w, L0_ffn_gate_bias, L0_ffn_w1, L0_ffn_w2, L0_ffn_w3, L0_ffn_w1s,
           L0_ffn_w2s, L0_ffn_w3s):
    import concourse.bacc as bacc
    from concourse.bass_utils import run_bass_kernel_spmd

    f = lambda a: np.asarray(a)
    images = f(x).reshape(IMAGES // 4, 2, 2, CHAN, SIDE, SIDE).swapaxes(1, 2)
    patches = images.reshape(IMAGES, CHAN, GRID, PATCH, GRID, PATCH).transpose(1, 3, 5, 0, 2, 4)
    qkv = f(L0_attn_w_qkv)
    params = _pack(PAR, PAR_W, 128, {
        "wtok": _chunks(f(L0_tok_W).T, 128),
        "wq": _chunks(_triples(qkv[:, 0:C]), HC),
        "wk": _chunks(_triples(qkv[:, C:2 * C]), HC),
        "wv": _chunks(qkv[:, 2 * C:], HC),
        "wproj": np.moveaxis(_triples(f(L0_attn_w_proj).T), 0, 2).transpose(1, 0, 2),
        "btok": _chunks(f(L0_tok_b), HC),
        "bproj": _chunks(f(L0_attn_b_proj), HC),
        "wgate": _chunks(f(L0_ffn_gate_w), HC),
        "temp": np.repeat(f(L0_attn_temperature).reshape(TRIPLES, HH).T, N, axis=0),
        "gbias": np.broadcast_to(f(L0_ffn_gate_bias), (128, E)),
    })
    head_of_row = np.full(RT, -1)
    for j in range(2):
        head_of_row[64 * j:64 * j + 48] = np.arange(48) // HD
    own = (head_of_row[:, None] == np.arange(HH)).astype(np.float32)
    consts = _pack(CON, CON_W, 128, {
        "ident": np.eye(128, dtype=np.float32),
        "before": np.triu(np.ones((TM, TM), np.float32), 1),
        "eye": np.tile(np.eye(N, dtype=np.float32), (HH, 1)),
        "qmask": own * np.float32(SCALE),
        "omask": own,
        "rank8": np.broadcast_to(np.arange(E, 0, -1, dtype=np.float32), (128, E)),
        "steps": np.broadcast_to(np.arange(SHT, dtype=np.float32) * XT, (128, SHT)),
        "tileno": np.broadcast_to(np.arange(RTILES, dtype=np.float32), (128, RTILES)),
    })
    w1 = np.concatenate([f(L0_ffn_w1), f(L0_ffn_w1s)[None]])
    w3 = np.concatenate([f(L0_ffn_w3), f(L0_ffn_w3s)[None]])
    w2 = np.concatenate([f(L0_ffn_w2), f(L0_ffn_w2s)[None]])
    w_up = np.stack([w1, w3], 1).reshape(E + 1, 2, 2, HC, I).transpose(0, 3, 1, 2, 4).reshape(E + 1, HC, UPF)
    w_down = w2.reshape(E + 1, IC, 128, C).transpose(0, 2, 1, 3).reshape(E + 1, 128, IC * C)
    arrays = {
        "xT": patches.reshape(KI, 128, TOKENS), "params": params, "consts": consts, "w_up": w_up, "w_down": w_down}
    arrays = {n: np.ascontiguousarray(a) for n, a in arrays.items()}

    nc = bacc.Bacc("TRN2", target_bir_lowering=False, num_devices=1)
    aps = {n: nc.dram_tensor(n, a.shape, F32, kind="ExternalInput").ap() for n, a in arrays.items()}
    out = nc.dram_tensor("out", (TOKENS, C), F32, kind="ExternalOutput").ap()
    xbuf = nc.dram_tensor("xbuf", (XROWS, C), F32, kind="Internal").ap()
    ybuf = nc.dram_tensor("ybuf", (XROWS, C), F32, kind="Internal").ap()
    build_program(nc, **aps, out=out, xbuf=xbuf, ybuf=ybuf)
    r = run_bass_kernel_spmd(nc, [arrays], core_ids=[0])
    return r.results[0]["out"].reshape(IMAGES, N, C)
```

```python
from contextlib import ExitStack

import numpy as np

import concourse.bass as bass
from concourse import mybir

ALU = mybir.AluOpType
ACT = mybir.ActivationFunctionType
AX = mybir.AxisListType
F32 = mybir.dt.float32
F16 = mybir.dt.float16
I32 = mybir.dt.int32

IMAGES, CHAN, SIDE, PATCH = 64, 3, 96, 16
GRID = SIDE // PATCH
N = GRID * GRID
TOKENS = IMAGES * N
D_IN = CHAN * PATCH * PATCH
C = 192
KI = D_IN // 128
HC = C // 2
HEADS, HD = 12, 16
HH = 3
TRIPLES = HEADS // HH
RT = 64 + HH * HD
ROWS = HH * N
G = 8
GT = G * N
GROUPS = IMAGES // G
TM = 96
GTILES = GT // TM
E, I = 8, 768
IC = I // 128
XT = 128
SHT = TOKENS // XT
RTILES = (2 * TOKENS + E * (XT - 1)) // XT
ALLT = SHT + RTILES
SH1 = 12
SCALE = HD ** -0.5
EPS = 1e-5
LIMIT = 10.0
SILU_LIMIT = LIMIT / (1.0 + float(np.exp(-LIMIT)))
BIG = 1e30

C1 = 128
C2 = C - C1
UPW = 2 * I
DNW = IC * C
STW = 2 * UPW + DNW
TAIL, MAIN, DOWN = 0, UPW, 2 * UPW
MAIN_LO, DOWN_LO = STW, STW + UPW
WF = STW + UPW + DNW
XS = 1024.0
HS = 256.0
WS = 2.0 ** 14
SILU_S, CLIP_HI, CLIP_LO, H_S, Y_S = range(5)
NSC = 5
ROUTE_G = 20
ROUTE_GS = 9


def _columns(fields):
    at, out = 0, {}
    for name, width in fields:
        out[name] = (at, at + width)
        at += width
    return out, at


PAR, PAR_W = _columns([
    ("wtok", KI * C), ("wq", 2 * 2 * RT), ("wk", 2 * 2 * RT), ("wv", 2 * C), ("wproj", 2 * C),
    ("btok", 2), ("bproj", 2), ("wgate", 2 * E), ("temp", TRIPLES), ("gbias", E)])
CON, CON_W = _columns([
    ("ident", 128), ("before", XT), ("eye", N), ("qmask", HH), ("omask", HH), ("rank8", E),
    ("steps", SHT), ("tileno", RTILES), ("upto", E * E), ("below", E * E)])


def build_program(nc, xT, params, consts, w_all, out, xbuf, dbuf, ybuf, rbuf):
    ctx = ExitStack()

    def sb(name, shape, dt=F32):
        return ctx.enter_context(nc.sbuf_tensor(name, shape, dt))

    def sem(name):
        return ctx.enter_context(nc.semaphore(name))

    with ctx:
        W16 = sb("W16", [128, (E + 1) * WF], F16)
        stage = sb("stage", [128, STW])
        par = sb("par", [128, PAR_W])
        con = sb("con", [128, CON_W])
        wsq = sb("wsq", [128, 2])
        wsum = sb("wsum", [128, 2])
        wstat = sb("wstat", [128, 4])
        wscale = sb("wscale", [128, 1])
        rscale = sb("rscale", [128, E + 1])
        shc = sb("shc", [128, NSC])
        tile_w = sb("tile_w", [1, RTILES], I32)
        sct = sb("sct", [128, NSC, RTILES])
        ones = sb("ones", [128, 1])
        mhalf = sb("mhalf", [128, 3 * E])
        phalf = sb("phalf", [TM, GTILES * E])
        rl = sb("rl", [TM, 12, GTILES * E])
        rtop = sb("rtop", [TM, 2, GTILES])
        rout = sb("rout", [TM, GTILES, 3, E])
        ones16 = sb("ones16", [128, XT], F16)
        before16 = sb("before16", [128, XT], F16)
        both = sb("both", [128, SHT * E], F16)
        pos = sb("pos", [XT, 2, SHT], I32)
        wgt = sb("wgt", [XT, 2, SHT])
        fstats = sb("fstats", [128, SHT, 6])
        fmv = sb("fmv", [128, SHT, 2])
        fve = sb("fve", [128, SHT])
        frs = sb("frs", [128, SHT])

        A_SIZES = [("xin", (128, KI, GT)), ("hT", (HC, 2, G, 64)), ("qblk", (RT, 2, G, ROWS)), ("kT", (RT, 2, GT)),
                   ("h0b", (HC, 2, GT)), ("vv", (128, 4, C)), ("S0", (ROWS, 16, 64)), ("S1", (ROWS, 16, 64)),
                   ("PT0", (128, 2, TRIPLES * ROWS)), ("PT1", (128, 2, TRIPLES * ROWS)), ("oT", (RT, 2, GT)),
                   ("tmask", (ROWS, 2, 2, N)), ("h1T", (HC, GTILES, 2, TM)), ("smax", (ROWS, 2, 16)),
                   ("ssum", (ROWS, 2, 16)), ("h1g", (TM, GTILES, C)), ("stats", (TM, GTILES, 6)),
                   ("mv", (TM, GTILES, 2)), ("veps", (TM, GTILES)), ("rstd", (TM, GTILES)), ("ntemp", (ROWS, TRIPLES))]
        arena_w = sum(int(np.prod(s[1:])) for _, s in A_SIZES)
        B_FROM = sum(int(np.prod(dict(A_SIZES)[n][1:])) for n in ("xin", "hT", "qblk", "kT", "h0b"))
        arena = sb("arena", [128, max(arena_w, B_FROM + 2 * SHT * C)])

        def view(v, shape):
            if len(shape) == 1:
                return v
            names = [f"d{i}" for i in range(len(shape))]
            return v.rearrange(f"p ({' '.join(names)}) -> p {' '.join(names)}", **dict(zip(names, shape)))

        a_at, at = {}, 0
        A = {}
        zero = arena[:, arena_w:arena_w + C]
        assert arena_w + C <= arena.shape[1]
        for name, shape in A_SIZES:
            n = int(np.prod(shape[1:]))
            a_at[name] = at
            A[name] = view(arena[0:shape[0], at:at + n], shape[1:])
            at += n
        xin, hT, qblk, kT, h0b, vv, oT, tmask, h1T = (A[n] for n in ("xin", "hT", "qblk", "kT", "h0b", "vv", "oT",
                                                                     "tmask", "h1T"))
        S, PT = [A["S0"], A["S1"]], [A["PT0"], A["PT1"]]
        smax, ssum, h1g, stats, mv, veps, rstd, ntemp = (A[n] for n in ("smax", "ssum", "h1g", "stats", "mv", "veps",
                                                                        "rstd", "ntemp"))

        def over(name, offset, shape, dt=F32):
            n = int(np.prod(shape)) * (2 if dt == F16 else 4) // 4
            v = arena[:, a_at[name] + offset:a_at[name] + offset + n]
            return view(v.bitcast(F16) if dt == F16 else v, shape)

        xt = over("xin", 0, (2, 2 * C1))
        xT16 = over("xin", 4 * C1, (2, 2, 2, XT), F16)
        sg = over("hT", 0, (I,))
        up = over("qblk", 0, (I,))
        hh = over("qblk", I, (I,))
        yy = over("kT", 0, (2, C))
        hhT = over("kT", 2 * C, (2, IC, XT), F16)
        h1 = over("vv", 0, (SHT, C))
        acc = over("vv", SHT * C, (SHT, C))
        assert a_at["vv"] == B_FROM and 2 * C + IC * XT <= a_at["vv"] - a_at["kT"]
        FS = STW // (2 * C)
        fin = view(stage[:, 0:FS * 2 * C], (FS, 2, C))

        SE = SHT * E

        def routing(at, *shape):
            return view(par[:, at:at + int(np.prod(shape))], shape)

        R3 = routing(0, SHT, 3, E)
        own_at = 3 * SE
        small_at = 9 * SE
        assert small_at + 3 * RTILES + 2 * SHT + 5 * E <= PAR["btok"][0] and RTILES * E <= 3 * SE

        bank = [ctx.enter_context(nc.psum_tensor(f"bank{i}", [128, 512], F32)) for i in range(8)]

        def P(name):
            a, b = PAR[name]
            return par[:, a:b]

        def K(name):
            a, b = CON[name]
            return con[:, a:b]

        wtok = P("wtok").rearrange("p (c n) -> p c n", c=KI)
        wq = P("wq").rearrange("p (c t n) -> p c t n", c=2, t=2)
        wk = P("wk").rearrange("p (c t n) -> p c t n", c=2, t=2)
        wv = P("wv").rearrange("p (c n) -> p c n", c=2)
        wproj = P("wproj").rearrange("p (t n) -> p t n", t=2)
        wgate = P("wgate").rearrange("p (c n) -> p c n", c=2)
        ident = K("ident")

        s_par = sem("params_in")
        s_xin = sem("group_in")
        s_zero = sem("zeroed")
        s_zfill = sem("dispatch_zeroed")
        s_tok = sem("tok_done")
        s_hT = sem("hT_ready")
        s_h0b = sem("h0b_ready")
        s_qk = sem("qk_done")
        s_q = sem("q_ready")
        s_k = sem("k_ready")
        s_vd = sem("v_done")
        s_v = sem("v_ready")
        s_S = sem("scores_done")
        s_sm = sem("scores_masked")
        s_mx = sem("max_ready")
        s_sub = sem("max_subtracted")
        s_ex = sem("exp_ready")
        s_sr = sem("sums_inverted")
        s_pn = sem("probs_ready")
        s_T = sem("probsT_done")
        s_PT = sem("probsT_ready")
        s_O = sem("heads_done")
        s_oT = sem("heads_ready")
        s_pj = sem("proj_done")
        s_var = sem("var_ready")
        s_rstd = sem("rstd_ready")
        s_h1 = sem("h1_ready")
        s_h1o = sem("h1_out")
        s_hTd = sem("h1T_done")
        s_h1T = sem("h1T_ready")
        s_lg = sem("logits_done")
        s_lgr = sem("logits_ready")
        s_ntemp = sem("temperature_mask")
        s_st = sem("stats_ready")
        s_ag = sem("mean_var_ready")
        s_su = sem("sums_ready")
        s_ext = sem("heads_partly_read")
        s_win = [sem(f"weights_in_{x}") for x in ("main", "tail")]
        s_wm = sem("weights_row_squares")
        s_wM = sem("weights_squares")
        s_wst = sem("weights_scale_steps")
        s_ws = sem("weights_scale")
        s_whi = sem("weights_hi")
        s_wlo = sem("weights_lo")
        s_ra = sem("softplus_act")
        s_rg = sem("choice_chain")
        s_rs = sem("sqrt_ready")
        s_rc = sem("choice_ready")
        s_rco = sem("choice_out")
        s_rlast = sem("last_choice_out")
        s_rin = sem("choices_in")
        s_route = sem("routing_chain")
        s_both = sem("both_choices")
        s_cnt = sem("counts_done")
        s_cntr = sem("counts_read")
        s_pos = sem("positions_ready")
        s_h1in = [sem(f"h1_in{q}") for q in range(3)]
        s_scat = sem("rows_dispatched")
        s_xl = [sem(f"x_in{i}") for i in range(2)]
        s_xd = sem("x_transposed")
        s_xh = sem("x_hi")
        s_xT = sem("x_lo")
        s_ud = sem("up_done")
        s_sg = sem("silu_ready")
        s_up = sem("up_clipped")
        s_h = sem("h_ready")
        s_hd = sem("h_transposed")
        s_hhi = sem("h_hi")
        s_hlo = sem("h_lo")
        s_yd = sem("y_done")
        s_y = sem("y_read")
        s_yo = [sem(f"y_out{i}") for i in range(2)]
        s_shc = sem("shared_scales")
        s_f = [sem(f"chosen_rows_in{i}") for i in range(FS)]
        s_fa = sem("rows_added")
        s_fst = sem("final_stats")
        s_fag = sem("final_mean_var")
        s_fv = sem("final_var")
        s_fr = sem("final_rstd")
        s_fn = sem("final_rows")
        s_fo = sem("output_stored")

        def wait_apart(eng, signal, count):
            count = count if isinstance(count, int) else eng.compute_val(count)
            eng.wait_ge(s_par, 32)
            eng.wait_ge(signal, count)

        def first(i):
            return isinstance(i, int) and i == 0

        def tiles_from(eng, lo, hi, body):
            if lo % 2:
                body(lo, 1)
                lo += 1
            if (hi - lo) // 2 > 0:
                with eng.Fori(0, (hi - lo) // 2) as it:
                    body(it * 2 + lo, 0)
                    body(it * 2 + (lo + 1), 1)
            if (hi - lo) % 2:
                body(hi - 1, 0)

        SH2 = SH1 + RTILES
        ZPART = RTILES // (GROUPS - 2)
        BATCHES = [(0, 6), (6, 12), (12, 18)]

        EMBED_AFTER = (2, 5, 8, 11, 13, 15)
        COUNT_AT = 3
        WEIGHTS_AT = COUNT_AT + 2
        STRAIGHT = SH1
        COMBINE_LAG = 3

        block = ctx.enter_context(nc.Block())

        @block.sync
        def _(sp):
            def load_group(g):
                sp.dma_start(xin, xT[:, :, bass.ds(g * GT, GT)].rearrange("c p n -> p c n")).then_inc(s_xin, 16)

            def load_main(e):
                sp.dma_start(stage[:, MAIN:STW], w_all[bass.ds(e, 1), :, MAIN:STW]
                             .rearrange("o p n -> p (o n)")).then_inc(s_win[0], 16)

            def load_tail(e):
                sp.dma_start(stage[:, TAIL:MAIN], w_all[bass.ds(e, 1), :, TAIL:MAIN]
                             .rearrange("o p n -> p (o n)")).then_inc(s_win[1], 16)

            def zero_rows(tile, tiles):
                sp.dma_start(dbuf[bass.ds(tile * XT, tiles * XT), :].rearrange("(t p) n -> p t n", p=128),
                             zero.rearrange("p (o n) -> p o n", o=1).to_broadcast([128, tiles, C])
                             ).then_inc(s_zfill, 16)

            def store_group(g):
                sp.wait_ge(s_h1, g * GTILES + GTILES)
                sp.dma_start(xbuf[bass.ds(g * GT, GT), :].rearrange("(t p) n -> p t n", p=TM),
                             h1g).then_inc(s_h1o, 16)

            def store_choice(g):
                sp.wait_ge(s_rc, g + 1)
                sp.dma_start(rbuf[bass.ds(g * GT, GT), :].rearrange("(t p) n -> p t n", p=TM),
                             rout[:, :, :, :].rearrange("p t w e -> p t (w e)")).then_inc(s_rco, 16)

            sp.dma_start(par[:, :], params).then_inc(s_par, 16)
            load_group(0)
            sp.dma_start(con[:, :], consts).then_inc(s_par, 16)
            load_main(0)
            load_tail(0)
            sp.wait_ge(s_tok, 2)
            load_group(1)
            sp.wait_ge(s_zero, 1)
            zero_rows(ZPART * (GROUPS - 2), RTILES - ZPART * (GROUPS - 2))

            def group(g, load=True, choice=True, store=True, tail=True):
                if load:
                    sp.wait_ge(s_tok, g * 2 + 4)
                    load_group(g + 2)
                wait_apart(sp, s_wlo, g * 2 + 1)
                load_main(g + 1)
                if tail:
                    wait_apart(sp, s_wlo, g * 2 + 2)
                    load_tail(g + 1)
                if choice:
                    zero_rows((g - 1) * ZPART, ZPART)
                    store_choice(g - 1)
                if store:
                    store_group(g)

            group(0, choice=False)
            with sp.Fori(1, GROUPS - 2) as g:
                group(g)
            group(GROUPS - 2, load=False)

            def load_x(buf, row, b):
                sp.dma_start(xt[:, b, 0:C], buf[bass.ds(row, XT), :]).then_inc(s_xl[b], 16)
                sp.dma_start(xt[:, b, C:2 * C1], buf[bass.ds(row, XT), C1:C]).then_inc(s_xl[b], 16)

            sp.wait_ge(s_tok, 2 * GROUPS)
            sp.wait_ge(s_h1o, 16 * (GROUPS - 1))
            load_x(xbuf, 0, 0)
            load_x(xbuf, XT, 1)
            group(GROUPS - 1, load=False, store=False, choice=False, tail=False)

            def load_h1(q):
                lo, hi = BATCHES[q]
                sp.dma_start(h1[:, lo:hi, :], xbuf[lo * XT:hi * XT, :].rearrange("(k p) n -> p k n", p=XT)
                             ).then_inc(s_h1in[q], 16)

            sp.wait_ge(s_xd, 1)
            load_x(xbuf, 2 * XT, 0)
            store_group(GROUPS - 1)
            store_choice(GROUPS - 2)
            sp.wait_ge(s_xd, 2)
            load_x(xbuf, 3 * XT, 1)
            sp.wait_ge(s_wlo, 2 * GROUPS)
            load_tail(GROUPS)
            sp.wait_ge(s_h1o, 16 * GROUPS)
            sp.wait_ge(s_lgr, GROUPS)
            sp.wait_ge(s_pj, GROUPS * GTILES)
            load_h1(0)
            sp.wait_ge(s_xd, 3)
            load_x(xbuf, 4 * XT, 0)
            load_h1(1)
            sp.wait_ge(s_xd, 4)
            load_x(xbuf, 5 * XT, 1)
            load_h1(2)

            def next_x(buf, skipped, store):
                def body(n, b):
                    sp.wait_ge(s_xd, n - 1)
                    load_x(buf, (n - skipped) * XT, b)
                    if store:
                        store_y(n - 4, b)
                return body

            def store_y(i, b):
                sp.wait_ge(s_y, i + 1)
                sp.dma_start(ybuf[bass.ds((i - SH1) * XT, XT), :], yy[:, b, :]).then_inc(s_yo[b], 16)

            routed, again = (dbuf, SH1), (xbuf, RTILES)
            tiles_from(sp, 6, SH1, next_x(xbuf, 0, False))
            sp.wait_ge(s_scat, 16 * 2 * SHT)
            tiles_from(sp, SH1, SH1 + 4, next_x(*routed, False))
            tiles_from(sp, SH1 + 4, SH2, next_x(*routed, True))
            tiles_from(sp, SH2, SH2 + 4, next_x(*again, True))
            tiles_from(sp, SH2 + 4, ALLT, next_x(*again, False))

            for q, (lo, hi) in enumerate(BATCHES):
                sp.wait_ge(s_fn, q + 1)
                sp.dma_start(out[lo * XT:hi * XT, :].rearrange("(k p) n -> p k n", p=XT),
                             acc[:, lo:hi, :]).then_inc(s_fo, 16)
            sp.wait_ge(s_fo, 16 * len(BATCHES))

        @block.tensor
        def _(pe):
            def embed(g, mt):
                def wait():
                    if mt == 0:
                        pe.wait_ge(s_xin, g * 16 + 16)
                    if not first(g):
                        pe.wait_ge(s_v, g * 2)

                def chunk(c):
                    if c == 0:
                        wait()
                    m = pe.matmul(bank[mt][0:HC, 0:GT], wtok[:, c, mt * HC:(mt + 1) * HC], xin[:, c, :],
                                  start=(c == 0), stop=(c == KI - 1))
                    if c == KI - 1:
                        m.then_inc(s_tok, 1)
                return chunk

            def project(g, x):
                if x == 0:
                    pe.wait_ge(s_hT, g * 2 + 2)
                elif not first(g):
                    pe.wait_ge(s_sm, g * 2)
                w, b0 = ((wq, 0), (wk, 6))[x]
                for tp in range(2):
                    for c in range(2):
                        m = pe.matmul(bank[b0 + tp][0:RT, 0:GT], w[0:HC, c, tp, :], hT[:, c, :, 0:N],
                                      start=(c == 0), stop=(c == 1))
                    m.then_inc(s_qk, 1)

            def values(g):
                pe.wait_ge(s_q, g * 2 + 2)
                for half in range(2):
                    for pair in range(2):
                        at = half * 4 + pair * 2
                        for c in range(2):
                            st = hT[:, c, at:at + 2, :].rearrange("p r m -> p (r m)")
                            m = pe.matmul(bank[half][:, pair * C:(pair + 1) * C], st, wv[0:HC, c, :],
                                          start=(c == 0), stop=(c == 1))
                    m.then_inc(s_vd, 1)

            def scores(g, h, between=None):
                if h == 0:
                    pe.wait_ge(s_q, g * 2 + 2)
                    pe.wait_ge(s_k, g * 2 + 2)
                n = 0
                for tp in range(2):
                    for b in range(4):
                        for j in range(2):
                            im, at = h * 4 + b, (tp * 4 + b) * N
                            m = pe.matmul(bank[4 + 2 * h + j][0:ROWS, at:at + N],
                                          qblk[64 * j:64 * j + 48, tp, im, :],
                                          kT[64 * j:64 * j + 48, tp, im * N:(im + 1) * N], start=True, stop=True)
                            n += 1
                            if n == 16:
                                m.then_inc(s_S, 1)
                            if between and n in EMBED_AFTER:
                                between(EMBED_AFTER.index(n))

            def probsT(g, h):
                wait_apart(pe, s_pn, g * 2 + h + 1)
                for pair in range(2):
                    for j in range(2):
                        for tp in range(2):
                            at = ((j * 2 + tp) * 2 + pair) * 2
                            src = S[h][:, at:at + 2, :].rearrange("p r m -> p (r m)")
                            m = pe.transpose(bank[2 + pair][:, (tp * 2 + j) * ROWS:(tp * 2 + j + 1) * ROWS],
                                             src, ident[0:ROWS, 0:ROWS])
                    m.then_inc(s_T, 1)

            def heads(g, h):
                pe.wait_ge(s_v, g * 2 + 2)
                if h == 1:
                    pe.wait_ge(s_oT, g * 4 + 2)
                else:
                    pe.wait_ge(s_sm, g * 2 + 1)
                wait_apart(pe, s_PT, g * 4 + 2 * h + 2)
                for r in range(2):
                    for tp in range(2):
                        for pair in range(2):
                            for j in range(2):
                                t = 2 * tp + j
                                at = (tp * 2 + pair) * ROWS
                                wide = 64 if j == 0 else 48
                                m = pe.matmul(bank[4 + r][64 * j:64 * j + wide, at:at + ROWS],
                                              vv[64 * r:64 * r + N, h * 2 + pair, t * 48:t * 48 + wide],
                                              PT[h][64 * r:64 * r + N, pair, t * ROWS:(t + 1) * ROWS],
                                              start=True, stop=True)
                    m.then_inc(s_O, 1)

            def proj(g):
                pe.wait_ge(s_oT, g * 4 + 4)
                pe.wait_ge(s_h0b, g + 1)
                for t in range(GTILES):
                    o = bank[6 + t // 2][0:TM, (t % 2) * C:(t % 2 + 1) * C]
                    for tp in range(2):
                        pe.matmul(o, oT[:, tp, t * TM:(t + 1) * TM], wproj[0:RT, tp, :],
                                  start=(tp == 0), stop=False, skip_group_check=True)
                    for c in range(2):
                        m = pe.matmul(o[:, c * HC:(c + 1) * HC], h0b[:, c, t * TM:(t + 1) * TM],
                                      ident[0:HC, 0:HC], start=False, stop=(c == 1), skip_group_check=True)
                    m.then_inc(s_pj, 1)

            def router_T(g, b0=2):
                pe.wait_ge(s_h1, g * GTILES + GTILES)
                for t in range(GTILES):
                    for c in range(2):
                        at = ((t % 2) * 2 + c) * TM
                        m = pe.transpose(bank[b0 + t // 2][0:HC, at:at + TM],
                                         h1g[:, t, c * HC:(c + 1) * HC], ident[0:TM, 0:TM])
                    if t > 0:
                        m.then_inc(s_hTd, 1)

            def router(g, b0=2):
                pe.wait_ge(s_h1T, g * 2 + 2)
                for t in range(GTILES):
                    for c in range(2):
                        m = pe.matmul(bank[b0 + 1][0:TM, 400 + t * E:400 + (t + 1) * E], h1T[:, t, c, :],
                                      wgate[0:HC, c, :], start=(c == 0), stop=(c == 1))
                m.then_inc(s_lg, 1)

            def counts(i):
                pe.wait_ge(s_both, 1)
                pe.wait_ge(s_xT, i + 2)
                o = bank[7][:, 2 * XT:2 * XT + SE + E]
                pe.matmul(o[:, 0:SE], before16[:, :], both[:, :], start=True, stop=False, skip_group_check=True)
                pe.matmul(o[:, SE:], ones16[:, :], both[:, SE - E:], start=False, stop=False, skip_group_check=True)
                for d in range(1, SHT + 1):
                    n = (SHT - d) * E if d > 1 else SE - E
                    if d > 1:
                        n += E
                    m = pe.matmul(o[:, d * E:d * E + n], ones16[:, :], both[:, 0:n], start=False, stop=(d == SHT),
                                  skip_group_check=True)
                m.then_inc(s_cnt, 1)

            def X(i, b):
                pe.wait_ge(s_xl[b], (i - b) * 16 + 32)
                if not first(i):
                    pe.wait_ge(s_xT, i)
                if isinstance(i, int) and i == COUNT_AT + 2:
                    pe.wait_ge(s_cntr, 1)
                for c in range(2):
                    m = pe.transpose(bank[7][:, c * XT:(c + 1) * XT], xt[:, b, c * C1:(c + 1) * C1], ident)
                m.then_inc(s_xd, 1)

            def U(i, b, off):
                pe.wait_ge(s_xT, i + 1)
                for n in range(2):
                    for k in range(2):
                        if not first(i):
                            pe.wait_ge(s_sg if k == 0 else s_up, i * 2 + n - 1)
                        col = k * I + n * (I // 2)
                        parts = ((0, 0, MAIN), (0, 0, MAIN_LO), (1, 0, MAIN), (0, 1, TAIL), (1, 1, TAIL))
                        for z, (lo, tail, at) in enumerate(parts):
                            m = pe.matmul(bank[2 * k + n][:, 0:I // 2], xT16[:, b, lo, tail, :],
                                          W16[:, bass.ds(off + at + col, I // 2)],
                                          start=(z == 0), stop=(z == len(parts) - 1))
                        m.then_inc(s_ud, 1)

            def H(i):
                for q in range(2):
                    pe.wait_ge(s_h, i * 2 + q + 1)
                    for c in range(3):
                        ic = q * 3 + c
                        m = pe.transpose(bank[4 + q][:, c * XT:(c + 1) * XT], hh[:, ic * 128:(ic + 1) * 128], ident)
                    m.then_inc(s_hd, 1)

            def D(i, off):
                pe.wait_ge(s_hlo, i * 2 + 2)
                if not first(i):
                    pe.wait_ge(s_y, i)
                for ic in range(IC):
                    for z, (lo, at) in enumerate(((0, DOWN), (0, DOWN_LO), (1, DOWN))):
                        m = pe.matmul(bank[6][:, 0:C], hhT[:, lo, ic, :], W16[:, bass.ds(off + at + ic * C, C)],
                                      start=(ic == 0 and z == 0), stop=(ic == IC - 1 and z == 2))
                m.then_inc(s_yd, 1)

            def shared(i):
                return 0

            def expert_of(i):
                return pe.value_load(tile_w[0:1, bass.ds(i - SH1, 1)], min_val=0, max_val=E * WF)

            def step(i, b, prev, cur, more=True, counting=False):
                prev, cur = prev(i - 1), cur(i)
                H(i - 1)
                if more:
                    X(i + 1, 1 - b)
                U(i, b, cur)
                if counting:
                    counts(i)
                D(i - 1, prev)

            pe.wait_ge(s_par, 32)
            pe.wait_ge(s_zero, 1)
            for mt in range(2):
                put = embed(0, mt)
                for c in range(KI):
                    put(c)
            project(0, 0)
            project(0, 1)
            values(0)

            def group(g, start=False, last=False):
                scores(g, 0, None if last else embed(g + 1, 0))
                if not start:
                    router_T(g - 1)
                scores(g, 1, None if last else embed(g + 1, 1))
                if not start:
                    router(g - 1)
                    pe.wait_ge(s_lgr, g)
                probsT(g, 0)
                if not last:
                    project(g + 1, 0)
                heads(g, 0)
                probsT(g, 1)
                if not last:
                    project(g + 1, 1)
                heads(g, 1)
                if not last:
                    values(g + 1)
                    pe.wait_ge(s_k, g * 2 + 4)
                else:
                    X(0, 0)
                    pe.wait_ge(s_xT, 1)
                proj(g)

            group(0, start=True)
            with pe.Fori(1, GROUPS - 1) as g:
                group(g)
            group(GROUPS - 1, last=True)
            U(0, 0, 0)
            router_T(GROUPS - 1, 4)
            X(1, 1)
            router(GROUPS - 1, 4)
            pe.wait_ge(s_lgr, GROUPS)
            for i in range(1, COUNT_AT + 2):
                step(i, i % 2, shared, shared, counting=(i == COUNT_AT))
            tiles_from(pe, COUNT_AT + 2, SH1, lambda i, b: step(i, b, shared, shared))
            pe.wait_ge(s_pos, 2)
            pe.wait_ge(s_wlo, 2 * (E + 1))
            step(SH1, 0, shared, expert_of)
            tiles_from(pe, SH1 + 1, SH2, lambda i, b: step(i, b, expert_of, expert_of))
            step(SH2, SH2 % 2, expert_of, shared)
            tiles_from(pe, SH2 + 1, ALLT - 1, lambda i, b: step(i, b, shared, shared))
            step(ALLT - 1, (ALLT - 1) % 2, shared, shared, more=False)
            H(ALLT - 1)
            D(ALLT - 1, 0)

        @block.scalar
        def _(act):
            AC = nc.scalar

            def hT_out(g):
                if not first(g):
                    act.wait_ge(s_h0b, g)
                for mt in range(2):
                    act.wait_ge(s_tok, g * 2 + mt + 1)
                    AC.activation(hT[:, mt, :, 0:N], bank[mt][0:HC, 0:GT].rearrange("p (b n) -> p b n", b=G),
                                  ACT.Identity, bias=P("btok")[0:HC, mt:mt + 1]).then_inc(s_hT, 1)

            def k_out(g):
                for tp in range(2):
                    act.wait_ge(s_qk, g * 4 + 3 + tp)
                    AC.copy(kT[:, tp, :], bank[6 + tp][0:RT, 0:GT]).then_inc(s_k, 1)

            def v_out(g):
                for half in range(2):
                    act.wait_ge(s_vd, g * 2 + half + 1)
                    AC.copy(vv[:, half * 2:half * 2 + 2, :],
                            bank[half][:, 0:2 * C].rearrange("p (a n) -> p a n", a=2)).then_inc(s_v, 1)

            def exps(g, h):
                act.wait_ge(s_sub, g * 2 + h + 1)
                AC.activation(S[h][:, :, 0:N], S[h][:, :, 0:N], ACT.Exp).then_inc(s_ex, 1)

            def probsT_out(g, h):
                for pair in range(2):
                    act.wait_ge(s_T, g * 4 + h * 2 + pair + 1)
                    AC.copy(PT[h][:, pair, :], bank[2 + pair][:, 0:TRIPLES * ROWS]).then_inc(s_PT, 1)

            def h1T_out(g, b0=2):
                act.wait_ge(s_hTd, g * 2 + 1)
                AC.copy(h1T[:, 0:2, :, :], bank[b0][0:HC, 0:4 * TM]
                        .rearrange("p (t c n) -> p t c n", t=2, c=2)).then_inc(s_h1T, 1)
                act.wait_ge(s_hTd, g * 2 + 2)
                AC.copy(h1T[:, 2, :, :], bank[b0 + 1][0:HC, 0:2 * TM]
                        .rearrange("p (c n) -> p c n", c=2)).then_inc(s_h1T, 1)

            def logits_out(g, b0=2):
                act.wait_ge(s_lg, g + 1)
                if not first(g):
                    act.wait_ge(s_rc, g)
                src = bank[b0 + 1][0:TM, 400:400 + GTILES * E]
                AC.activation(rl[:, 1, :], src, ACT.Abs).then_inc(s_ra, 1)
                AC.copy(rl[:, 0, :], src).then_inc(s_lgr, 1)
                act.wait_ge(s_ra, g * 3 + 1)
                AC.activation(rl[:, 2, :], rl[:, 1, :], ACT.Exp, scale=-1.0).then_inc(s_ra, 1)

            def softplus_ln(g):
                act.wait_ge(s_ra, g * 3 + 2)
                AC.activation(rl[:, 3, :], rl[:, 2, :], ACT.Ln, bias=ones[0:TM, 0:1]).then_inc(s_ra, 1)

            def weights_hi(e, parts=(0, 1)):
                wait_apart(act, s_ws, e + 1)
                for part in parts:
                    a, b = ((MAIN, STW), (TAIL, MAIN))[part]
                    AC.activation(W16[:, bass.ds(e * WF + a, b - a)], stage[:, a:b], ACT.Copy,
                                  scale=wscale[:, 0:1]).then_inc(s_whi, 1)

            def weights_squares(e):
                for i, (a, b) in enumerate(((MAIN, STW), (TAIL, MAIN))):
                    wait_apart(act, s_win[i], e * 16 + 16)
                    AC.activation(W16[:, bass.ds(e * WF + a, b - a)], stage[:, a:b], ACT.Square,
                                  accum_out=wsq[:, i:i + 1]).then_inc(s_wm, 1)

            def group(g, start=False, last=False):
                exps(g, 0)
                if not start:
                    h1T_out(g - 1)
                weights_hi(g, (0,))
                if not last:
                    hT_out(g + 1)
                if not start:
                    logits_out(g - 1)
                exps(g, 1)
                probsT_out(g, 0)
                if not start:
                    softplus_ln(g - 1)
                weights_hi(g, (1,))
                probsT_out(g, 1)
                if not last:
                    k_out(g + 1)
                    v_out(g + 1)
                    weights_squares(g + 1)

            def scale(i, c):
                if isinstance(i, int) and (i < SH1 or i >= SH2):
                    return shc[:, c:c + 1]
                return sct[:, c, bass.ds(i - SH1, 1)]

            def x_hi(i, b):
                act.wait_ge(s_xd, i + 1)
                AC.activation(xT16[:, b, 0, :, :], bank[7][:, 0:2 * XT].rearrange("p (c n) -> p c n", c=2),
                              ACT.Copy, scale=XS).then_inc(s_xh, 1)

            def silu(i, col):
                for n in range(2):
                    if not first(i):
                        act.wait_ge(s_h, i * 2 + n - 1)
                    wait_apart(act, s_ud, i * 4 + 2 * n + 1)
                    AC.activation(sg[:, n * (I // 2):(n + 1) * (I // 2)], bank[n][:, 0:I // 2], ACT.Silu,
                                  scale=col).then_inc(s_sg, 1)

            def h_hi(i, col):
                for q in range(2):
                    wait_apart(act, s_hd, i * 2 + q + 1)
                    AC.activation(hhT[:, 0, q * 3:q * 3 + 3, :], bank[4 + q][:, 0:3 * XT]
                                  .rearrange("p (c n) -> p c n", c=3), ACT.Copy, scale=col).then_inc(s_hhi, 1)

            def y_out(i, b, reused=True):
                if reused:
                    act.wait_ge(s_yo[b], (i - (SH1 + b)) * 8)
                wait_apart(act, s_yd, i + 1)
                AC.activation(yy[:, b, :], bank[6][:, 0:C], ACT.Copy, scale=scale(i, Y_S)).then_inc(s_y, 1)

            def step(i, b, prev, cur, more=True):
                h_hi(i - 1, scale(i - 1, H_S) if prev else shc[:, H_S:H_S + 1])
                if more:
                    x_hi(i + 1, 1 - b)
                silu(i, scale(i, SILU_S) if cur else shc[:, SILU_S:SILU_S + 1])

            act.wait_ge(s_par, 32)
            act.wait_ge(s_zero, 1)
            hT_out(0)
            k_out(0)
            v_out(0)
            weights_squares(0)
            group(0, start=True)
            group(1)
            with act.Fori(2, GROUPS - 1) as g:
                group(g)
            group(GROUPS - 1, last=True)
            x_hi(0, 0)
            act.wait_ge(s_shc, 1)
            silu(0, shc[:, SILU_S:SILU_S + 1])
            h1T_out(GROUPS - 1, 4)
            x_hi(1, 1)
            logits_out(GROUPS - 1, 4)
            h_hi(0, shc[:, H_S:H_S + 1])
            softplus_ln(GROUPS - 1)
            x_hi(2, 0)
            silu(1, shc[:, SILU_S:SILU_S + 1])
            for i in range(2, WEIGHTS_AT):
                if i == COUNT_AT:
                    weights_squares(E)
                step(i, i % 2, False, False)
            weights_hi(E)
            tiles_from(act, WEIGHTS_AT, SH1, lambda i, b: step(i, b, False, False))
            act.wait_ge(s_pos, 2)
            step(SH1, 0, False, True)
            for i in (SH1 + 1, SH1 + 2):
                step(i, i % 2, True, True)
                y_out(i - 1, (i - 1) % 2, reused=False)

            def routed(i, b):
                step(i, b, True, True)
                y_out(i - 1, 1 - b)

            tiles_from(act, SH1 + 3, SH2, routed)
            step(SH2, SH2 % 2, True, False)
            y_out(SH2 - 1, (SH2 - 1) % 2)
            tiles_from(act, SH2 + 1, ALLT - 1, lambda i, b: step(i, b, False, False))
            step(ALLT - 1, (ALLT - 1) % 2, False, False, more=False)
            h_hi(ALLT - 1, shc[:, H_S:H_S + 1])

        @block.vector
        def _(dve):
            V = nc.vector

            def q_out(g):
                for tp in range(2):
                    dve.wait_ge(s_qk, g * 4 + 1 + tp)
                    src = bank[tp][0:RT, 0:GT].rearrange("p (b o n) -> p b o n", b=G, o=1).to_broadcast([RT, G, HH, N])
                    msk = K("qmask")[0:RT].rearrange("p (o h u) -> p o h u", o=1, u=1).to_broadcast([RT, G, HH, N])
                    V.tensor_tensor(qblk[:, tp].rearrange("p b (h n) -> p b h n", h=HH), src, msk,
                                    ALU.mult).then_inc(s_q, 1)

            def mask_max(g, h):
                dve.wait_ge(s_S, g * 2 + h + 1)
                s = S[h][:, :, 0:N]
                for j in range(2):
                    m = V.tensor_tensor(S[h][:, j * 8:j * 8 + 8, 0:N].rearrange("p (t b) m -> p t b m", t=2),
                                        bank[4 + 2 * h + j][0:ROWS, 0:8 * N].rearrange("p (t b m) -> p t b m", t=2, b=4),
                                        tmask[:, j].rearrange("p t (o m) -> p t o m", o=1)
                                        .to_broadcast([ROWS, 2, 4, N]), ALU.mult)
                m.then_inc(s_sm, 1)
                dve.wait_ge(s_sm, g * 2 + h + 1)
                V.tensor_reduce(smax[:, h, :], s, AX.X, ALU.max).then_inc(s_mx, 1)
                dve.wait_ge(s_mx, g * 2 + h + 1)
                V.tensor_tensor(s, s, smax[:, h, :].rearrange("p (s o) -> p s o", o=1).to_broadcast([ROWS, 16, N]),
                                ALU.subtract).then_inc(s_sub, 1)

            def sums(g, h):
                dve.wait_ge(s_ex, g * 2 + h + 1)
                V.tensor_reduce(ssum[:, h, :], S[h][:, :, 0:N], AX.X, ALU.add).then_inc(s_su, 1)
                dve.wait_ge(s_su, g * 2 + h + 1)
                V.reciprocal(ssum[:, h, :], ssum[:, h, :]).then_inc(s_sr, 1)

            def heads_out(g, h, between=lambda: None):
                for r in range(2):
                    dve.wait_ge(s_O, g * 4 + h * 2 + r + 1)
                for k in range(HH):
                    for r in range(2):
                        src = bank[4 + r][0:RT, 0:4 * ROWS].rearrange("p (t a x) -> p t a x", t=2, a=2)[:, :, :, k * N:(k + 1) * N]
                        at = (h * 4 + r * 2) * N
                        dst = oT[:, :, at:at + 2 * N].rearrange("p t (a n) -> p t a n", a=2)
                        msk = K("omask")[0:RT, k:k + 1]
                        if k == 0:
                            V.tensor_scalar(dst, src, msk, None, ALU.mult).then_inc(s_ext, 1)
                        else:
                            dve.wait_ge(s_ext, g * 8 + h * 4 + (k - 1) * 2 + r + 1)
                            V.scalar_tensor_tensor(out=dst, in0=src, scalar=msk, in1=dst, op0=ALU.mult,
                                                   op1=ALU.add).then_inc(s_ext if k < HH - 1 else s_oT, 1)
                        between()

            def norm(g, between):
                for t in range(GTILES):
                    dve.wait_ge(s_pj, g * GTILES + min(2 * (t // 2) + 2, GTILES))
                    V.bn_stats(stats[:, t, :], bank[6 + t // 2][0:TM, (t % 2) * C:(t % 2 + 1) * C]).then_inc(s_st, 1)
                    between()
                for t in range(GTILES):
                    wait_apart(dve, s_st, g * GTILES + t + 1)
                    V.bn_aggr(mv[:, t, :], stats[:, t, :]).then_inc(s_ag, 1)
                    between()
                dve.wait_ge(s_ag, g * GTILES + GTILES)
                V.tensor_scalar(veps, mv[:, :, 1], EPS, None, ALU.add).then_inc(s_var, 1)
                between(3)
                dve.wait_ge(s_rstd, g + 1)
                if not first(g):
                    dve.wait_ge(s_h1o, g * 16)
                    dve.wait_ge(s_hTd, g * 2)
                for t in range(GTILES):
                    V.tensor_scalar(h1g[:, t, :], bank[6 + t // 2][0:TM, (t % 2) * C:(t % 2 + 1) * C],
                                    mv[:, t, 0:1], rstd[:, t:t + 1], ALU.subtract, ALU.mult).then_inc(s_h1, 1)

            def choice(g):
                n = [0]

                def before():
                    dve.wait_ge(s_rg, g * ROUTE_G + n[0])

                def step(ins):
                    n[0] += 1
                    ins.then_inc(s_rg, 1)

                e, ln, d, z, sp = (rl[:, i, :] for i in (2, 3, 4, 5, 6))
                cube = lambda i: rl[:, i, :].rearrange("p (t e) -> p t e", t=GTILES)
                over_t = lambda v: v.rearrange("p (o e) -> p o e", o=1).to_broadcast([TM, GTILES, E])
                over_e = lambda v: v.rearrange("p (t o) -> p t o", o=1).to_broadcast([TM, GTILES, E])
                dve.wait_ge(s_lgr, g + 1)
                dve.wait_ge(s_ra, g * 3 + 3)
                step(V.tensor_scalar(d, e, 1.0, -1.0, ALU.add, ALU.add))
                yield
                before()
                step(V.tensor_scalar(z, d, 0.0, None, ALU.is_equal))
                yield
                before()
                step(V.tensor_tensor(d, d, z, ALU.add))
                yield
                before()
                step(V.reciprocal(d, d))
                yield
                step(V.tensor_tensor(z, z, e, ALU.mult))
                yield
                before()
                step(V.tensor_tensor(d, d, e, ALU.mult))
                yield
                before()
                step(V.tensor_tensor(d, d, ln, ALU.mult))
                yield
                before()
                step(V.tensor_tensor(d, d, z, ALU.add))
                yield
                before()
                step(V.scalar_tensor_tensor(out=sp, in0=rl[:, 0, :], scalar=0.0, in1=d, op0=ALU.max, op1=ALU.add))
                assert n[0] == ROUTE_GS
                yield
                dve.wait_ge(s_rs, g + 1)
                step(V.tensor_tensor(cube(7), rout[:, :, 2, :], over_t(P("gbias")[0:TM]), ALU.add))
                for c in range(2):
                    yield
                    before()
                    step(V.tensor_reduce(rtop[:, 0, :], cube(7), AX.X, ALU.max))
                    yield
                    before()
                    step(V.tensor_tensor(cube(8), cube(7), over_e(rtop[:, 0, :]), ALU.is_equal))
                    yield
                    before()
                    step(V.tensor_tensor(cube(8), cube(8), over_t(K("rank8")[0:TM]), ALU.mult))
                    yield
                    before()
                    step(V.tensor_reduce(rtop[:, 1, :], cube(8), AX.X, ALU.max))
                    yield
                    before()
                    m = V.tensor_tensor(rout[:, :, c, :], cube(8), over_e(rtop[:, 1, :]), ALU.is_equal)
                    if c == 0:
                        step(m)
                        yield
                        before()
                        step(V.scalar_tensor_tensor(out=cube(7), in0=rout[:, :, 0, :], scalar=-BIG, in1=cube(7),
                                                    op0=ALU.mult, op1=ALU.add))
                    else:
                        m.then_inc(s_rc, 1)
                assert n[0] == ROUTE_G

            def weights_scale(e):
                dve.wait_ge(s_wM, e + 1)
                V.tensor_tensor(wstat[:, 0:1], wsum[:, 0:1], wsum[:, 1:2], ALU.add).then_inc(s_wst, 1)
                dve.wait_ge(s_wst, e * 5 + 1)
                V.tensor_scalar(wstat[:, 0:1], wstat[:, 0:1], 2.0 ** -120, None, ALU.max).then_inc(s_wst, 1)
                dve.wait_ge(s_wst, e * 5 + 2)
                V.tensor_scalar(wstat[:, 1:2].bitcast(I32), wstat[:, 0:1].bitcast(I32), 1, 0x3F800000,
                                ALU.logical_shift_right, ALU.bitwise_and).then_inc(s_wst, 1)
                dve.wait_ge(s_wst, e * 5 + 3)
                V.tensor_scalar(wstat[:, 2:3], wstat[:, 1:2], 2.0 ** 64, None, ALU.mult).then_inc(s_wst, 1)
                dve.wait_ge(s_wst, e * 5 + 4)
                V.tensor_copy(rscale[:, bass.ds(e, 1)], wstat[:, 2:3])
                V.reciprocal(wstat[:, 3:4], wstat[:, 2:3]).then_inc(s_wst, 1)
                dve.wait_ge(s_wst, e * 5 + 5)
                V.tensor_scalar(wscale[:, 0:1], wstat[:, 3:4], WS, None, ALU.mult).then_inc(s_ws, 1)

            def weights_lo_main(e):
                dve.wait_ge(s_whi, e * 2 + 1)
                V.scalar_tensor_tensor(out=W16[:, bass.ds(e * WF + STW, UPW + DNW)], in0=stage[:, MAIN:STW],
                                       scalar=wscale[:, 0:1], in1=W16[:, bass.ds(e * WF + MAIN, UPW + DNW)],
                                       op0=ALU.mult, op1=ALU.subtract).then_inc(s_wlo, 1)

            def weights_lo_tail(e):
                dve.wait_ge(s_whi, e * 2 + 2)
                tail = W16[C2:128, bass.ds(e * WF + TAIL, UPW)]
                V.scalar_tensor_tensor(out=tail, in0=stage[C2:128, TAIL:MAIN], scalar=wscale[C2:128, 0:1], in1=tail,
                                       op0=ALU.mult, op1=ALU.subtract).then_inc(s_wlo, 1)

            def scale_columns(cols, r, q, done):
                V.tensor_scalar(cols(SILU_S), r, 1.0 / (XS * WS), None, ALU.mult)
                V.tensor_scalar(cols(CLIP_HI), q, LIMIT * XS * WS, None, ALU.mult)
                V.tensor_scalar(cols(CLIP_LO), q, -LIMIT * XS * WS, None, ALU.mult)
                V.tensor_scalar(cols(H_S), r, HS / (XS * WS), None, ALU.mult)
                V.tensor_scalar(cols(Y_S), r, 1.0 / (HS * WS), None, ALU.mult).then_inc(done, 1)

            def group(g, start=False, last=False):
                steps = iter(()) if start else choice(g - 1)

                def between(count=1):
                    for _ in range(count):
                        next(steps, None)

                mask_max(g, 0)
                weights_scale(g)
                sums(g, 0)
                mask_max(g, 1)
                sums(g, 1)
                weights_lo_main(g)
                between(2)
                heads_out(g, 0)
                between()
                if not last:
                    q_out(g + 1)
                between(2)
                weights_lo_tail(g)
                between(4)
                heads_out(g, 1)
                if last:
                    x_lo(0, 0)
                norm(g, between)
                between(ROUTE_G)

            def scale(i, c):
                return sct[:, c, bass.ds(i - SH1, 1)]

            def x_lo(i, b):
                dve.wait_ge(s_xh, i + 1)
                V.scalar_tensor_tensor(out=xT16[:, b, 1, :, :], in0=bank[7][:, 0:2 * XT].rearrange("p (c n) -> p c n", c=2),
                                       scalar=XS, in1=xT16[:, b, 0, :, :], op0=ALU.mult, op1=ALU.subtract).then_inc(s_xT, 1)

            def h_lo(i, col):
                for q in range(2):
                    dve.wait_ge(s_hhi, i * 2 + q + 1)
                    V.scalar_tensor_tensor(out=hhT[:, 1, q * 3:q * 3 + 3, :], in0=bank[4 + q][:, 0:3 * XT]
                                           .rearrange("p (c n) -> p c n", c=3), scalar=col,
                                           in1=hhT[:, 0, q * 3:q * 3 + 3, :], op0=ALU.mult,
                                           op1=ALU.subtract).then_inc(s_hlo, 1)

            def up_h(i, hi, lo):
                for n in range(2):
                    part = slice(n * (I // 2), (n + 1) * (I // 2))
                    dve.wait_ge(s_ud, i * 4 + 2 * n + 2)
                    V.tensor_scalar(up[:, part], bank[2 + n][:, 0:I // 2], hi, lo, ALU.min, ALU.max).then_inc(s_up, 1)
                    dve.wait_ge(s_up, i * 2 + n + 1)
                    dve.wait_ge(s_sg, i * 2 + n + 1)
                    if not first(i):
                        dve.wait_ge(s_hd, i * 2)
                    V.scalar_tensor_tensor(out=hh[:, part], in0=sg[:, part], scalar=SILU_LIMIT, in1=up[:, part],
                                           op0=ALU.min, op1=ALU.mult).then_inc(s_h, 1)

            def y_add(i, t):
                dve.wait_ge(s_yd, i + 1)
                V.scalar_tensor_tensor(out=acc[:, bass.ds(t, 1), :].rearrange("p o n -> p (o n)"), in0=bank[6][:, 0:C],
                                       scalar=shc[:, Y_S:Y_S + 1],
                                       in1=h1[:, bass.ds(t, 1), :].rearrange("p o n -> p (o n)"),
                                       op0=ALU.mult, op1=ALU.add).then_inc(s_y, 1)

            def step(i, b, prev, cur, more=True, aside=None):
                h_lo(i - 1, scale(i - 1, H_S) if prev else shc[:, H_S:H_S + 1])
                if more:
                    x_lo(i + 1, 1 - b)
                if aside:
                    aside()
                if cur:
                    up_h(i, scale(i, CLIP_HI), scale(i, CLIP_LO))
                else:
                    up_h(i, shc[:, CLIP_HI:CLIP_HI + 1], shc[:, CLIP_LO:CLIP_LO + 1])

            dve.wait_ge(s_par, 32)
            V.tensor_copy(before16[:, :], K("before"))
            V.tensor_scalar(ntemp, P("temp")[0:ROWS], -1.0, None, ALU.mult).then_inc(s_ntemp, 1)
            dve.wait_ge(s_ntemp, 1)
            for tp in range(2):
                for j in range(2):
                    t = 2 * tp + j
                    V.tensor_scalar(tmask[:, j, tp, :], K("eye")[0:ROWS], ntemp[:, t:t + 1], 1.0,
                                    ALU.mult, ALU.add).then_inc(s_ntemp, 1)
            dve.wait_ge(s_ntemp, 5)
            dve.wait_ge(s_zero, 1)
            q_out(0)
            group(0, start=True)
            scale_columns(lambda c: shc[:, c:c + 1], wstat[:, 2:3], wstat[:, 3:4], s_shc)
            with dve.Fori(1, GROUPS - 1) as g:
                group(g)
            group(GROUPS - 1, last=True)

            n = [0]

            def link(ins, wait=True):
                n[0] += 1
                ins.then_inc(s_route, 1)
                if wait:
                    dve.wait_ge(s_route, n[0])

            flat = lambda i: routing(3 * SE + i * SE, SE)
            cube = lambda i: routing(3 * SE + i * SE, SHT, E)
            over_k = lambda v: v.rearrange("p (o e) -> p o e", o=1).to_broadcast([XT, SHT, E])
            chosen = [R3[:, :, c, :] for c in range(2)]
            score = R3[:, :, 2, :]
            ends, nt, base = (routing(small_at + i * E, E) for i in range(3))
            posf = [routing(small_at + 3 * E + i * SHT, SHT) for i in range(2)]

            def both_choices():
                dve.wait_ge(s_rin, 16)
                V.tensor_tensor(both[:, :].rearrange("p (k e) -> p k e", k=SHT), chosen[0], chosen[1],
                                ALU.add).then_inc(s_both, 1)

            def positions():
                dve.wait_ge(s_cnt, 1)
                rows = routing(3 * SE, SHT + 1, E)
                V.tensor_copy(rows.rearrange("p k e -> p (k e)"), bank[7][:, 2 * XT:2 * XT + SE + E]).then_inc(s_cntr, 1)
                dve.wait_ge(s_cntr, 1)
                count = rows[:, SHT, :]
                ge, sq = cube(2).rearrange("p k e -> p (k e)").rearrange("p (e s) -> p e s", e=E), routing(3 * SE + 3 * SE, E, E)
                link(V.tensor_tensor(ge, count.rearrange("p (e o) -> p e o", o=1).to_broadcast([XT, E, SHT]),
                                     K("steps").rearrange("p (o s) -> p o s", o=1).to_broadcast([XT, E, SHT]), ALU.is_gt))
                link(V.tensor_reduce(nt, ge, AX.X, ALU.add))
                link(V.tensor_tensor(sq, nt.rearrange("p (o f) -> p o f", o=1).to_broadcast([XT, E, E]),
                                     K("below").rearrange("p (e f) -> p e f", e=E), ALU.mult))
                link(V.tensor_reduce(base, sq, AX.X, ALU.add))
                link(V.tensor_tensor(rows[:, 0:SHT, :], rows[:, 0:SHT, :], over_k(base), ALU.add))
                for c in range(2):
                    link(V.tensor_tensor(cube(2 + c), chosen[c], rows[:, 0:SHT, :], ALU.mult), wait=(c == 1))
                for c in range(2):
                    link(V.tensor_reduce(posf[c], cube(2 + c), AX.X, ALU.add), wait=(c == 1))
                for c in range(2):
                    m = V.tensor_copy(pos[:, c, :], posf[c])
                m.then_inc(s_pos, 1)

            def tile_tables():
                sq = routing(3 * SE + 3 * SE, E, E)
                link(V.tensor_tensor(sq, nt.rearrange("p (o f) -> p o f", o=1).to_broadcast([XT, E, E]),
                                     K("upto").rearrange("p (e f) -> p e f", e=E), ALU.mult))
                link(V.tensor_reduce(ends, sq, AX.X, ALU.add))
                own, hot = routing(own_at, RTILES, E), routing(own_at + RTILES * E, RTILES, E)
                idx, r, q = (routing(small_at + 3 * E + 2 * SHT + i * RTILES, RTILES) for i in range(3))
                over = lambda v: v.rearrange("p (o e) -> p o e", o=1).to_broadcast([XT, RTILES, E])
                per = lambda v: v.rearrange("p (t o) -> p t o", o=1).to_broadcast([XT, RTILES, E])
                link(V.tensor_tensor(own, over(ends), per(K("tileno")), ALU.is_le))
                link(V.tensor_reduce(idx, own, AX.X, ALU.add))
                link(V.tensor_scalar(idx, idx, float(E - 1), None, ALU.min))
                link(V.tensor_scalar(r[0:1], idx[0:1], float(WF), float(WF), ALU.mult, ALU.add))
                link(V.tensor_copy(tile_w[:, :], r[0:1]))
                link(V.tensor_scalar(idx, idx, -1.0, float(E), ALU.mult, ALU.add))
                link(V.tensor_tensor(hot, over(K("rank8")), per(idx), ALU.is_equal))
                dve.wait_ge(s_ws, E + 1)
                link(V.tensor_tensor(hot, hot, over(rscale[:, 1:E + 1]), ALU.mult))
                link(V.tensor_reduce(r, hot, AX.X, ALU.add))
                link(V.reciprocal(q, r))
                scale_columns(lambda c: sct[:, c, :], r, q, s_pos)

            def weights_of_choices():
                for c in range(2):
                    link(V.tensor_tensor(cube(4), chosen[c], score, ALU.mult))
                    link(V.tensor_reduce(wgt[:, c, :], cube(4), AX.X, ALU.add))
                link(V.tensor_tensor(posf[0], wgt[:, 0, :], wgt[:, 1, :], ALU.add))
                link(V.tensor_scalar(posf[0], posf[0], 1e-6, None, ALU.max))
                link(V.reciprocal(posf[0], posf[0]))
                for c in range(2):
                    link(V.tensor_tensor(wgt[:, c, :], wgt[:, c, :], posf[0], ALU.mult))

            CLIPS = shc[:, CLIP_HI:CLIP_HI + 1], shc[:, CLIP_LO:CLIP_LO + 1]
            up_h(0, *CLIPS)
            x_lo(1, 1)
            steps = choice(GROUPS - 1)

            def choose(count):
                for _ in range(count):
                    next(steps, None)

            step(1, 1, False, False, aside=lambda: choose(ROUTE_GS))
            dve.wait_ge(s_h1in[0], 16)
            y_add(0, 0)
            step(2, 0, False, False, aside=lambda: choose(ROUTE_G))
            y_add(1, 1)
            for i in range(3, STRAIGHT):
                if i == 6:
                    for q in (1, 2):
                        dve.wait_ge(s_h1in[q], 16)
                step(i, i % 2, False, False)
                if i == COUNT_AT:
                    both_choices()
                    positions()
                y_add(i - 1, i - 1)
                if i == COUNT_AT + 1:
                    weights_scale(E)
                elif i == COUNT_AT + 2:
                    weights_lo_main(E)
                elif i == COUNT_AT + 3:
                    weights_lo_tail(E)
                elif i == COUNT_AT + 4:
                    tile_tables()
                elif i == COUNT_AT + 5:
                    weights_of_choices()

            def shared(i, b):
                step(i, b, False, False)
                y_add(i - 1, i - 1)

            tiles_from(dve, STRAIGHT, SH1, shared)
            dve.wait_ge(s_pos, 2)
            step(SH1, 0, False, True)
            y_add(SH1 - 1, SH1 - 1)
            tiles_from(dve, SH1 + 1, SH2, lambda i, b: step(i, b, True, True))

            def combine(pair):
                ks = (2 * pair, 2 * pair + 1)
                rows = [acc[:, k, :] for k in ks]
                for k in ks:
                    dve.wait_ge(s_f[k % FS], 32 * (k // FS + 1))
                dve.wait_ge(s_y, ks[1] + 1 if ks[1] < SH1 else ks[1] + 1 + RTILES)
                for c in range(2):
                    for k, row in zip(ks, rows):
                        if c == 1:
                            dve.wait_ge(s_fa, 2 * ks[0] + k % 2 + 1)
                        V.scalar_tensor_tensor(out=row, in0=fin[:, k % FS, c, :], scalar=wgt[:, c, k:k + 1], in1=row,
                                               op0=ALU.mult, op1=ALU.add).then_inc(s_fa, 1)
                for k, row in zip(ks, rows):
                    dve.wait_ge(s_fa, 2 * ks[0] + k % 2 + 3)
                    V.bn_stats(fstats[:, k, :], row).then_inc(s_fst, 1)
                for k in ks:
                    dve.wait_ge(s_fst, k + 1)
                    V.bn_aggr(fmv[:, k, :], fstats[:, k, :]).then_inc(s_fag, 1)
                for q, (lo, hi) in enumerate(BATCHES):
                    if ks[1] == hi - 1:
                        dve.wait_ge(s_fag, hi)
                        V.tensor_scalar(fve[:, lo:hi], fmv[:, lo:hi, 1], EPS, None, ALU.add).then_inc(s_fv, 1)

            def final_norm(q):
                dve.wait_ge(s_fr, q + 1)
                for k in range(*BATCHES[q]):
                    m = V.tensor_scalar(acc[:, k, :], acc[:, k, :], fmv[:, k, 0:1], frs[:, k:k + 1],
                                        ALU.subtract, ALU.mult)
                m.then_inc(s_fn, 1)

            pair, normed = 0, 0

            def combine_next():
                nonlocal pair, normed
                combine(pair)
                pair += 1
                if 2 * pair == BATCHES[normed][1] + 2:
                    final_norm(normed)
                    normed += 1

            for i in range(SH2, ALLT):
                step(i, i % 2, i == SH2, False, more=(i < ALLT - 1))
                if i > SH2:
                    y_add(i - 1, i - 1 - RTILES)
                if i - SH2 >= COMBINE_LAG:
                    combine_next()
            h_lo(ALLT - 1, shc[:, H_S:H_S + 1])
            while 2 * pair < SHT - 2:
                combine_next()
            y_add(ALLT - 1, SHT - 1)
            combine_next()
            while normed < len(BATCHES):
                final_norm(normed)
                normed += 1

        @block.gpsimd
        def _(pool):
            PO = nc.gpsimd
            for v, x in ((hT[:, :, :, N:64], 0.0), (S[0][:, :, N:64], 0.0), (S[1][:, :, N:64], 0.0),
                         (zero, 0.0), (ones[:, :], 1.0), (ones16[:, :], 1.0), (phalf[:, :], 0.5), (mhalf[:, :], -0.5)):
                m = PO.memset(v, x)
            m.then_inc(s_zero, 1)
            pool.wait_ge(s_zero, 1)
            pool.wait_ge(s_par, 32)

            def h0b_out(g):
                before = None if first(g) else pool.compute_val(g * GTILES)
                wait_apart(pool, s_hT, g * 2 + 2)
                if before is not None:
                    pool.wait_ge(s_pj, before)
                for mt in range(2):
                    for half in range(2):
                        m = PO.tensor_scalar(
                            h0b[:, mt, half * 4 * N:(half + 1) * 4 * N].rearrange("p (r a n) -> p r a n", r=2, a=2),
                            hT[:, mt, half * 4:half * 4 + 4, 0:N].rearrange("p (a r) n -> p r a n", a=2),
                            P("bproj")[0:HC, mt:mt + 1], None, ALU.add)
                m.then_inc(s_h0b, 1)

            def normalise(g, h):
                pool.wait_ge(s_sr, g * 2 + h + 1)
                s = S[h][:, :, 0:N]
                PO.tensor_tensor(s, s, ssum[:, h, :].rearrange("p (s o) -> p s o", o=1).to_broadcast([ROWS, 16, N]),
                                 ALU.mult).then_inc(s_pn, 1)

            def weights_sum(e):
                wait_apart(pool, s_wm, e * 2 + 2)
                PO.partition_all_reduce(wsum[:, :], wsq[:, :], 128, bass.bass_isa.ReduceOp.add).then_inc(s_wM, 1)

            def scores_sqrt(g):
                pool.wait_ge(s_rg, g * ROUTE_G + ROUTE_GS)
                if not first(g):
                    wait_apart(pool, s_rco, g * 16)
                PO.tensor_tensor(rout[:, :, 2, :], rl[:, 6, :].rearrange("p (t e) -> p t e", t=GTILES),
                                 phalf[:, :].rearrange("p (t e) -> p t e", t=GTILES), ALU.pow).then_inc(s_rs, 1)

            def group(g, start=False, last=False):
                normalise(g, 0)
                normalise(g, 1)
                if not start:
                    scores_sqrt(g - 1)
                pool.wait_ge(s_var, g + 1)
                PO.tensor_tensor(rstd, veps, mhalf[0:TM, 0:GTILES], ALU.pow).then_inc(s_rstd, 1)
                if not last:
                    weights_sum(g + 1)
                    h0b_out(g + 1)

            h0b_out(0)
            weights_sum(0)
            group(0, start=True)
            group(1)
            with pool.Fori(2, GROUPS - 1) as g:
                group(g)
            group(GROUPS - 1, last=True)
            scores_sqrt(GROUPS - 1)
            pool.wait_ge(s_rc, GROUPS)
            PO.dma_start(rbuf[(GROUPS - 1) * GT:TOKENS, :].rearrange("(t p) n -> p t n", p=TM),
                         rout[:, :, :, :].rearrange("p t w e -> p t (w e)")).then_inc(s_rlast, 16)
            pool.wait_ge(s_rlast, 16)
            pool.wait_ge(s_rco, 16 * (GROUPS - 1))
            pool.wait_ge(s_pj, GROUPS * GTILES)
            PO.dma_start(R3.rearrange("p k w e -> p k (w e)"),
                         rbuf.rearrange("(k p) n -> p k n", p=XT)).then_inc(s_rin, 16)
            weights_sum(E)

            for q in range(3):
                pool.wait_ge(s_h1in[q], 16)
            pool.wait_ge(s_zfill, 16 * (GROUPS - 1))
            pool.wait_ge(s_pos, 1)
            for k in range(SHT):
                for c in range(2):
                    PO.indirect_dma_start(dbuf[:, :], bass.IndirectOffsetOnAxis(ap=pos[:, c, k:k + 1], axis=0),
                                          h1[:, k, :], None).then_inc(s_scat, 16)

            def final_rstd(q):
                lo, hi = BATCHES[q]
                pool.wait_ge(s_fv, q + 1)
                PO.tensor_tensor(frs[:, lo:hi], fve[:, lo:hi], mhalf[:, 0:hi - lo], ALU.pow).then_inc(s_fr, 1)

            pool.wait_ge(s_wlo, 2 * (E + 1))
            for b in range(2):
                pool.wait_ge(s_yo[b], 16 * ((RTILES + 1 - b) // 2))
            for k in range(SHT):
                if k >= FS:
                    pool.wait_ge(s_fa, 4 * ((k - FS) // 2) + 4)
                for c in range(2):
                    PO.indirect_dma_start(fin[:, k % FS, c, :], None, ybuf[:, :],
                                          bass.IndirectOffsetOnAxis(ap=pos[:, c, k:k + 1], axis=0)
                                          ).then_inc(s_f[k % FS], 16)
                if k == SHT - 3:
                    final_rstd(0)
            for q in range(1, len(BATCHES)):
                final_rstd(q)


def _pack(columns, width, rows, fields):
    out = np.zeros((rows, width), np.float32)
    for name, v in fields.items():
        a, b = columns[name]
        out[:v.shape[0], a:b] = v.reshape(v.shape[0], b - a)
    return out


def _triples(w):
    w = w.reshape(*w.shape[:-1], 2, 2, HH * HD)
    out = np.zeros((*w.shape[:-3], 2, RT), np.float32)
    out[..., 0:48] = w[..., 0, :]
    out[..., 64:112] = w[..., 1, :]
    return out


def _chunks(w, p):
    return np.moveaxis(w.reshape(-1, p, *w.shape[1:]), 0, 1)


def kernel(x, L0_tok_W, L0_tok_b, L0_attn_w_qkv, L0_attn_w_proj, L0_attn_b_proj, L0_attn_temperature,
           L0_ffn_input_ids, L0_ffn_gate_w, L0_ffn_gate_bias, L0_ffn_w1, L0_ffn_w2, L0_ffn_w3, L0_ffn_w1s,
           L0_ffn_w2s, L0_ffn_w3s):
    import concourse.bacc as bacc
    from concourse.bass_utils import run_bass_kernel_spmd

    f = lambda a: np.asarray(a)
    images = f(x).reshape(IMAGES // 4, 2, 2, CHAN, SIDE, SIDE).swapaxes(1, 2)
    patches = images.reshape(IMAGES, CHAN, GRID, PATCH, GRID, PATCH).transpose(1, 3, 5, 0, 2, 4)
    qkv = f(L0_attn_w_qkv)
    params = _pack(PAR, PAR_W, 128, {
        "wtok": _chunks(f(L0_tok_W).T, 128),
        "wq": _chunks(_triples(qkv[:, 0:C]), HC),
        "wk": _chunks(_triples(qkv[:, C:2 * C]), HC),
        "wv": _chunks(qkv[:, 2 * C:], HC),
        "wproj": np.moveaxis(_triples(f(L0_attn_w_proj).T), 0, 2).transpose(1, 0, 2),
        "btok": _chunks(f(L0_tok_b), HC),
        "bproj": _chunks(f(L0_attn_b_proj), HC),
        "wgate": _chunks(f(L0_ffn_gate_w), HC),
        "temp": np.repeat(f(L0_attn_temperature).reshape(TRIPLES, HH).T, N, axis=0),
        "gbias": np.broadcast_to(f(L0_ffn_gate_bias), (128, E)),
    })
    head_of_row = np.full(RT, -1)
    for j in range(2):
        head_of_row[64 * j:64 * j + 48] = np.arange(48) // HD
    own = (head_of_row[:, None] == np.arange(HH)).astype(np.float32)
    consts = _pack(CON, CON_W, 128, {
        "ident": np.eye(128, dtype=np.float32),
        "before": np.triu(np.ones((XT, XT), np.float32), 1),
        "eye": np.tile(np.eye(N, dtype=np.float32), (HH, 1)),
        "qmask": own * np.float32(SCALE),
        "omask": own,
        "rank8": np.broadcast_to(np.arange(E, 0, -1, dtype=np.float32), (128, E)),
        "steps": np.broadcast_to(np.arange(SHT, dtype=np.float32) * XT, (128, SHT)),
        "tileno": np.broadcast_to(np.arange(RTILES, dtype=np.float32), (128, RTILES)),
        "upto": np.broadcast_to(np.tril(np.ones((E, E), np.float32)).reshape(-1), (128, E * E)),
        "below": np.broadcast_to(np.tril(np.full((E, E), XT, np.float32), -1).reshape(-1), (128, E * E)),
    })
    w1 = np.concatenate([f(L0_ffn_w1s)[None], f(L0_ffn_w1)])
    w3 = np.concatenate([f(L0_ffn_w3s)[None], f(L0_ffn_w3)])
    w2 = np.concatenate([f(L0_ffn_w2s)[None], f(L0_ffn_w2)])
    w_up = np.concatenate([w1, w3], 2)
    tail = np.concatenate([w_up[:, C1:], w_up[:, C1:]], 1)
    down = w2.reshape(E + 1, IC, 128, C).transpose(0, 2, 1, 3).reshape(E + 1, 128, DNW)
    arrays = {
        "xT": patches.reshape(KI, 128, TOKENS), "params": params, "consts": consts,
        "w_all": np.concatenate([tail, w_up[:, :C1], down], 2)}
    arrays = {n: np.ascontiguousarray(a) for n, a in arrays.items()}

    nc = bacc.Bacc("TRN2", target_bir_lowering=False, num_devices=1)
    aps = {n: nc.dram_tensor(n, a.shape, F32, kind="ExternalInput").ap() for n, a in arrays.items()}
    out = nc.dram_tensor("out", (TOKENS, C), F32, kind="ExternalOutput").ap()
    rows = RTILES * XT
    xbuf = nc.dram_tensor("xbuf", (TOKENS, C), F32, kind="Internal").ap()
    dbuf = nc.dram_tensor("dbuf", (rows, C), F32, kind="Internal").ap()
    ybuf = nc.dram_tensor("ybuf", (rows, C), F32, kind="Internal").ap()
    rbuf = nc.dram_tensor("rbuf", (TOKENS, 3 * E), F32, kind="Internal").ap()
    build_program(nc, **aps, out=out, xbuf=xbuf, dbuf=dbuf, ybuf=ybuf, rbuf=rbuf)
    r = run_bass_kernel_spmd(nc, [arrays], core_ids=[0])
    return r.results[0]["out"].reshape(IMAGES, N, C)
```
